# Optimizing a Trainium2 kernel written in Bass

```python
import numpy as np
import jax
import jax.numpy as jnp

def _softmax(x, axis=-1):
    return jax.nn.softmax(x, axis=axis)

def _gelu(x):
    return jax.nn.gelu(x, approximate=True)

def _silu(x):
    return jax.nn.silu(x)

def _sigmoid(x):
    return jax.nn.sigmoid(x)

def _layernorm(x, axis=-1, eps=1e-05):
    m = jnp.mean(x, axis=axis, keepdims=True)
    v = jnp.var(x, axis=axis, keepdims=True)
    return (x - m) / jnp.sqrt(v + eps)

def _scatter_add(tgt, idx, src, axis=0):
    return tgt.at[idx].add(src)

def _segment_sum(src, seg, n):
    return jax.ops.segment_sum(src, seg, n)
kernel_name = 'mk_adj_ffn_d1_adj_r2_ceec9e'

def setup_inputs(seed: int=0):
    np.random.seed(seed)
    _w = jnp.asarray

    def _rec_inputs():
        import jax
        import jax.numpy as jnp
        _gk = jax.random.key(seed)
        x = -0.0005207 + 1.001 * jax.random.normal(jax.random.fold_in(_gk, 1), (8192, 128), jnp.float32)
        _a = jax.random.bernoulli(jax.random.fold_in(_gk, 2), 0.00195312, (8192, 8192))
        _a = jnp.logical_or(_a, jnp.swapaxes(_a, -1, -2))
        _a = jnp.logical_or(_a, jnp.eye(8192, dtype=bool))
        _af = _a.astype(jnp.float32)
        _af = _af * jax.random.uniform(jax.random.fold_in(_gk, 3), (8192, 8192), jnp.float32, 0.05, 2.05)
        adj = _af
        return (x, adj)
    x, adj = _rec_inputs()

    def _L0_gnn_setup():
        import jax, jax.numpy as jnp
        import numpy as np
        N = 4096
        D = 128
        CUTOFF = 1.0
        MU = 1.0
        SIGMA = 0.5

        def sensitivity(r, mu, sigma):
            return jnp.exp(-(1.0 / r - 1.0 / mu) ** 2 / (2.0 * sigma * sigma))
        key = jax.random.key(seed)
        k_z, k_d, k_w = jax.random.split(key, 3)
        z = jax.random.normal(k_z, (N, D), dtype=jnp.float32)
        dist_matrix = jax.random.uniform(k_d, (N, N), dtype=jnp.float32) * 2.0 + 0.05
        W = jax.random.normal(k_w, (D, D), dtype=jnp.float32)
        B = jnp.zeros((D,), dtype=jnp.float32)
        return {'z': z, 'dist_matrix': dist_matrix, 'W': W, 'B': B}
    _L0_gnn_all = _L0_gnn_setup()
    _L0_gnn_in = {k: v for k, v in _L0_gnn_all.items() if k in ('W', 'B')}
    del _L0_gnn_all

    def _L0_ffn_setup():
        import jax, jax.numpy as jnp
        import numpy as np
        B, S, H, F, E, K = (8, 2048, 128, 256, 16, 2)
        EPS = 1e-05
        key = jax.random.key(seed)
        ks = jax.random.split(key, 9)
        sc = 0.02
        return {'x': jax.random.normal(ks[0], (B, S, H), dtype=jnp.float32), 'gate_w': jax.random.normal(ks[1], (H, E), dtype=jnp.float32) * sc, 'gate_b': jnp.zeros((E,), dtype=jnp.float32), 'w1': jax.random.normal(ks[2], (E, H, F), dtype=jnp.float32) * sc, 'b1': jnp.zeros((E, F), dtype=jnp.float32), 'w2': jax.random.normal(ks[3], (E, F, H), dtype=jnp.float32) * sc, 'b2': jnp.zeros((E, H), dtype=jnp.float32), 'gamma': jnp.ones((H,), dtype=jnp.float32), 'beta': jnp.zeros((H,), dtype=jnp.float32)}
    _L0_ffn_all = _L0_ffn_setup()
    _L0_ffn_in = {k: v for k, v in _L0_ffn_all.items() if k in ('gate_w', 'gate_b', 'w1', 'b1', 'w2', 'b2', 'gamma', 'beta')}
    del _L0_ffn_all
    return {'x': x, 'adj': adj, 'L0_gnn_W': _L0_gnn_in['W'], 'L0_gnn_B': _L0_gnn_in['B'], 'L0_ffn_gate_w': _L0_ffn_in['gate_w'], 'L0_ffn_gate_b': _L0_ffn_in['gate_b'], 'L0_ffn_w1': _L0_ffn_in['w1'], 'L0_ffn_b1': _L0_ffn_in['b1'], 'L0_ffn_w2': _L0_ffn_in['w2'], 'L0_ffn_b2': _L0_ffn_in['b2'], 'L0_ffn_gamma': _L0_ffn_in['gamma'], 'L0_ffn_beta': _L0_ffn_in['beta']}

def reference(x, adj, L0_gnn_W, L0_gnn_B, L0_ffn_gate_w, L0_ffn_gate_b, L0_ffn_w1, L0_ffn_b1, L0_ffn_w2, L0_ffn_b2, L0_ffn_gamma, L0_ffn_beta):
    import jax
    import jax.numpy as jnp

    def _L0_gnn_ref(z, dist_matrix, W, B):
        import jax, jax.numpy as jnp
        import numpy as np
        N = 4096
        D = 128
        CUTOFF = 1.0
        MU = 1.0
        SIGMA = 0.5

        def sensitivity(r, mu, sigma):
            return jnp.exp(-(1.0 / r - 1.0 / mu) ** 2 / (2.0 * sigma * sigma))
        msg = z @ W + B
        sens = sensitivity(dist_matrix, MU, SIGMA)
        weights = jnp.where(dist_matrix < CUTOFF, sens, 0.0)
        return weights @ msg

    def _L0_ffn_ref(x, gate_w, gate_b, w1, b1, w2, b2, gamma, beta):
        import jax, jax.numpy as jnp
        import numpy as np
        B, S, H, F, E, K = (8, 2048, 128, 256, 16, 2)
        EPS = 1e-05
        gate_logits = x @ gate_w + gate_b
        topk_vals, topk_idx = jax.lax.top_k(gate_logits, K)
        topk_w = jax.nn.softmax(topk_vals, axis=-1)
        h = jax.nn.relu(jnp.einsum('bsh,ehf->bsef', x, w1) + b1)
        expert_out = jnp.einsum('bsef,efh->bseh', h, w2) + b2
        sel = jnp.take_along_axis(expert_out, topk_idx[:, :, :, None], axis=2)
        moe = jnp.sum(topk_w[..., None] * sel, axis=2)
        y = x + moe
        mu = jnp.mean(y, axis=-1, keepdims=True)
        var = jnp.var(y, axis=-1, keepdims=True)
        return (y - mu) / jnp.sqrt(var + EPS) * gamma + beta
    x = x + _L0_gnn_ref(_layernorm(x, axis=-1), adj, L0_gnn_W, L0_gnn_B)
    x = x + _L0_ffn_ref(_layernorm(x, axis=-1)[None], L0_ffn_gate_w, L0_ffn_gate_b, L0_ffn_w1, L0_ffn_b1, L0_ffn_w2, L0_ffn_b2, L0_ffn_gamma, L0_ffn_beta)[0]
    return x

_drawn_inputs = setup_inputs


def setup_inputs(seed=0):
    import zlib

    import numpy as np

    out = dict(_drawn_inputs(seed))
    spreads = {'L0_gnn_B': (0.0, 0.335),
     'L0_ffn_gate_b': (0.0, 0.8),
     'L0_ffn_b1': (0.0, 2.0),
     'L0_ffn_b2': (0.0, 2.0),
     'L0_ffn_gamma': (1.0, 0.6),
     'L0_ffn_beta': (0.0, 0.8)}
    factors = {'L0_ffn_gate_w': 8.0, 'L0_ffn_w1': 8.0, 'L0_ffn_w2': 8.0}
    for name, (base, spread) in spreads.items():
        noise = np.random.default_rng([zlib.crc32(name.encode()), seed]).standard_normal(out[name].shape)
        drawn = base * np.exp(spread * noise) if base else spread * noise
        out[name] = jnp.asarray(drawn.astype(out[name].dtype))
    for name, factor in factors.items():
        out[name] = (out[name] * factor).astype(out[name].dtype)
    return out
```

```python
import concourse.bass as bass
from concourse import mybir
from contextlib import ExitStack

F32 = mybir.dt.float32
I32 = mybir.dt.int32
U32 = mybir.dt.uint32
ALU = mybir.AluOpType
ACT = mybir.ActivationFunctionType

P = 128
EPS = 1e-5
TINY = 1e-18
RSQRT_BITS = 1597463007.0
RSQRT_STEPS = 3


def gnn_moe_kernel(nc, x, adj, gnn_w, gnn_b, gate_w, gate_b, w1, b1, w2, b2, gamma, beta, out):
    N, D = x.shape
    E, _, F = w1.shape
    FT = F // P
    TB = 4
    ROWS = TB * P
    GROUPS = N // ROWS
    JC = 1024
    CHUNKS = N // JC
    RING = 4
    PAIRS = JC // (2 * P)
    PPG = CHUNKS * PAIRS
    WSLOTS = 4
    HALF = TB // 2

    adj_v = adj.rearrange("(g b p) j -> p g b j", b=TB, p=P)
    out_v = out.rearrange("(g b p) d -> p g b d", b=TB, p=P)
    x_v = x.rearrange("(t p) d -> p t d", p=P)

    ctx = ExitStack()
    with ctx:
        def sb(name, shape, dt=F32):
            return ctx.enter_context(nc.sbuf_tensor(name, shape, dt))

        def sem(name):
            return ctx.enter_context(nc.semaphore(name))

        chunk = sb("chunk", [P, RING, TB, JC])
        wT = sb("wT", [P, WSLOTS, 2 * ROWS])
        msg = sb("msg", [P, N // P, D])
        xs = sb("xs", [P, N // P, D])
        w1s = sb("w1s", [P, E, F])
        w2s = sb("w2s", [P, E, FT, D])
        b1s = sb("b1s", [P, E, FT])
        b2s = sb("b2s", [E, D])
        gws = sb("gws", [P, E])
        wgs = sb("wgs", [P, D])
        bg_bc = sb("bg_bc", [P, D])
        gb_bc = sb("gb_bc", [P, E])
        gamma_bc = sb("gamma_bc", [P, D])
        beta_bc = sb("beta_bc", [P, D])
        ident = sb("ident", [P, P])
        tiny = sb("tiny", [P, 1])
        minus2 = sb("minus2", [P, 1])
        carrier = sb("carrier", [1, 2])
        iota_e = sb("iota_e", [P, E])
        accT = sb("accT", [P, ROWS])
        x1 = sb("x1", [P, TB, D])
        y = sb("y", [P, TB, D])
        yT = sb("yT", [P, ROWS])
        h = sb("h", [P, 2, FT, ROWS])
        fin = sb("fin", [P, TB, D])
        stats = sb("stats", [P, TB, 6])
        mv = sb("mv", [P, TB, 2])
        var = sb("var", [P, TB])
        rstd = sb("rstd", [P, TB])
        nt = sb("nt", [P, TB])
        logits = sb("logits", [P, TB, E])
        top8 = sb("top8", [P, TB, 8])
        idx8 = sb("idx8", [P, TB, 8], U32)
        idxf = sb("idxf", [P, TB, 2])
        dv = sb("dv", [P, TB])
        ed = sb("ed", [P, TB])
        p1 = sb("p1", [P, TB])
        p2 = sb("p2", [P, TB])
        ga = sb("ga", [P, TB, E])
        gates = sb("gates", [P, TB, E])
        gatesT = sb("gatesT", [E, ROWS])

        tp = [ctx.enter_context(nc.psum_tensor(f"tp{i}", [P, 2 * ROWS], F32)) for i in range(2)]
        acc = ctx.enter_context(nc.psum_tensor("acc", [P, ROWS], F32))
        yp = [ctx.enter_context(nc.psum_tensor(f"yp{i}", [P, ROWS], F32)) for i in range(2)]
        misc = ctx.enter_context(nc.psum_tensor("misc", [P, ROWS], F32))

        loaded = [sem(f"chunk_loaded{i}") for i in range(RING)]
        weights_in = sem("weights_in")
        x_in = sem("x_in")
        masked = sem("masked")
        logged = sem("logged")
        inverted = sem("inverted")
        squared = sem("squared")
        turned = sem("turned")
        weighted = sem("weighted")
        added = sem("added")
        accT_out = sem("accT_out")
        ident_zero = sem("ident_zero")
        const_ok = sem("const_ok")
        vec = sem("vector_step")
        sca = sem("scalar_step")
        ln_ready = sem("ln_ready")
        misc_full = sem("misc_full")
        misc_read = sem("misc_read")
        hid_full = sem("hid_full")
        hid_act0 = sem("hid_act0")
        hid_act1 = sem("hid_act1")
        y_full = sem("y_full")
        y_read = sem("y_read")
        diff_ready = sem("diff_ready")
        exp_ready = sem("exp_ready")
        fin_ready = sem("fin_ready")
        stored = sem("stored")
        fin_free = sem("fin_free")

        block = ctx.enter_context(nc.Block())

        W_DMAS = 11
        CONSTS = 5
        MISC = 5
        SETUP_MISC = 2

        @block.sync
        def _(sp):
            sp.dma_start(xs[:, :, :], x_v).then_inc(x_in, 16)

            def load(g, c):
                sp.dma_start(chunk[:, c % RING, :, :],
                             adj_v[:, g, :, c * JC:(c + 1) * JC]).then_inc(loaded[c % RING], 16)

            for dst, src in ((wgs[:, :], gnn_w), (gws[:, :], gate_w),
                             (w1s[:, :, :], w1.rearrange("e h f -> h e f")),
                             (w2s[:, :, :, :], w2.rearrange("e (t f) h -> f e t h", t=FT)),
                             (b2s[:, :], b2),
                             (bg_bc[:, :], gnn_b.rearrange("(a d) -> a d", a=1).partition_broadcast(P)),
                             (gb_bc[:, :], gate_b.rearrange("(a d) -> a d", a=1).partition_broadcast(P)),
                             (gamma_bc[:, :], gamma.rearrange("(a d) -> a d", a=1).partition_broadcast(P)),
                             (beta_bc[:, :], beta.rearrange("(a d) -> a d", a=1).partition_broadcast(P))):
                sp.dma_start(dst, src).then_inc(weights_in, 16)
            for t in range(FT):
                with nc.allow_non_contiguous_dma(reason="one word per partition, once"):
                    sp.dma_start(b1s[:, :, t:t + 1],
                                 b1[:, t * P:(t + 1) * P].rearrange("e (f a) -> f e a", a=1)).then_inc(weights_in, 16)
            for c in range(RING):
                load(0, c)

            def group(g, last):
                for c in range(CHUNKS):
                    if last and c + RING >= CHUNKS:
                        break
                    sp.wait_ge(turned, (g * CHUNKS + c + 1) * PAIRS)
                    n = c + RING
                    load(g + n // CHUNKS, n % CHUNKS)

            with sp.Fori(0, GROUPS - 1) as g:
                group(g, False)
            group(GROUPS - 1, True)

        @block.gpsimd
        def _(pool):
            pool.memset(ident[:, :], 0.0).then_inc(ident_zero, 1)
            pool.memset(tiny[:, :], TINY).then_inc(const_ok, 1)
            pool.iota(iota_e[:, :], pattern=[[1, E]], base=0, channel_multiplier=0,
                      allow_small_or_imprecise_dtypes=True).then_inc(const_ok, 1)
            pool.wait_ge(ident_zero, 1)
            pool.affine_select(out=ident[:, :], in_=ident[:, :], compare_op=ALU.not_equal, fill=1.0,
                               base=0, pattern=[[-1, P]], channel_multiplier=1).then_inc(const_ok, 1)

            pool.sem_inc(fin_free, 1)
            with pool.Fori(0, GROUPS) as g:
                pool.wait_ge(fin_ready, g + 1)
                pool.dma_start(out_v[:, g, :, :], fin[:, :, :]).then_inc(stored, 16)
                pool.wait_ge(stored, (g + 1) * 16)
                pool.sem_inc(fin_free, 1)
            pool.wait_ge(stored, GROUPS * 16)

        @block.scalar
        def _(act):
            act.preload_act_table_set("natural_log_exp_and_others")
            act.sem_inc(weighted, 2)
            act.wait_ge(const_ok, CONSTS)

            def half(c, hb):
                return chunk[:, c % RING, hb * HALF:(hb + 1) * HALF, :]

            def log_half(g, c, hb):
                act.wait_ge(masked, (g * CHUNKS + c) * 2 + hb + 1)
                act.activation(half(c, hb), half(c, hb), ACT.Ln, bias=tiny[:, 0:1]).then_inc(logged, 1)

            def invert_half(g, c, hb):
                act.wait_ge(logged, (g * CHUNKS + c) * 2 + hb + 1)
                act.activation(half(c, hb), half(c, hb), ACT.Exp, scale=-1.0).then_inc(inverted, 1)

            def weigh(g, m):
                act.wait_ge(turned, g * PPG + m + 1)
                act.wait_ge(added, g * PPG + m + 1)
                act.activation(wT[:, m % WSLOTS, :], tp[m % 2][:, :], ACT.Exp, bias=minus2[:, 0:1],
                               scale=-2.0).then_inc(weighted, 1)

            def group(g, last):
                for c in range(CHUNKS):
                    n = c + 2
                    ahead = [lambda: log_half(g + n // CHUNKS, n % CHUNKS, 0),
                             lambda: log_half(g + n // CHUNKS, n % CHUNKS, 1),
                             lambda: invert_half(g + n // CHUNKS, n % CHUNKS, 0),
                             lambda: invert_half(g + n // CHUNKS, n % CHUNKS, 1)]
                    for k in range(PAIRS):
                        weigh(g, c * PAIRS + k)
                        if not (last and n >= CHUNKS):
                            ahead[k]()
                act.wait_ge(diff_ready, g + 1)
                act.activation(ed[:, :], dv[:, :], ACT.Exp).then_inc(exp_ready, 1)
                for e in range(E):
                    act.wait_ge(hid_full, g * E + e + 1)
                    act.wait_ge(y_full, g * E + e + 1)
                    act.activation(h[:, e % 2, 0, :], tp[e % 2][:, 0:ROWS], ACT.Relu,
                                   bias=b1s[:, e, 0:1]).then_inc(hid_act0, 1)

            for c in range(2):
                for hb in range(2):
                    log_half(0, c, hb)
                for hb in range(2):
                    invert_half(0, c, hb)
            with act.Fori(0, GROUPS - 1) as g:
                group(g, False)
            group(GROUPS - 1, True)

        @block.vector
        def _(dve):
            steps = [0]

            def plain_next():
                dve.tensor_copy(carrier[0:1, 1:2], carrier[0:1, 0:1])

            def link(ins, base, plain=False):
                steps[0] += 1
                ins.then_inc(vec, 1)
                dve.wait_ge(vec, base + steps[0])
                if plain:
                    plain_next()

            def half(c, hb):
                return chunk[:, c % RING, hb * HALF:(hb + 1) * HALF, :]

            def mask_half(g, c, hb):
                if hb == 0:
                    dve.wait_ge(loaded[c % RING], (g * (CHUNKS // RING) + c // RING + 1) * 16)
                dve.scalar_tensor_tensor(out=half(c, hb), in0=half(c, hb), scalar=1.0, in1=half(c, hb),
                                         op0=ALU.is_lt, op1=ALU.mult).then_inc(masked, 1)

            def square_half(g, c, hb):
                dve.wait_ge(inverted, (g * CHUNKS + c) * 2 + hb + 1)
                dve.scalar_tensor_tensor(out=half(c, hb), in0=half(c, hb), scalar=2.0, in1=half(c, hb),
                                         op0=ALU.subtract, op1=ALU.mult).then_inc(squared, 1)

            def rows_norm(src, dst, base, last_inc=None):
                for b in range(TB):
                    ins = dve.bn_stats(stats[:, b, :], src[:, b, :])
                link(ins, base, plain=True)
                for b in range(TB):
                    ins = dve.bn_aggr(mv[:, b, :], stats[:, b, :])
                link(ins, base)
                link(dve.tensor_scalar(var[:, :], mv[:, :, 1], EPS, None, ALU.add), base)
                link(dve.tensor_scalar(rstd[:, :].bitcast(I32), var[:, :].bitcast(I32), -0.5, RSQRT_BITS,
                                       ALU.mult, ALU.add), base)
                for _ in range(RSQRT_STEPS):
                    link(dve.tensor_tensor(nt[:, :], rstd[:, :], rstd[:, :], ALU.mult), base)
                    link(dve.tensor_tensor(nt[:, :], nt[:, :], var[:, :], ALU.mult), base)
                    link(dve.tensor_scalar(nt[:, :], nt[:, :], -0.5, 1.5, ALU.mult, ALU.add), base)
                    link(dve.tensor_tensor(rstd[:, :], rstd[:, :], nt[:, :], ALU.mult), base)
                for b in range(TB):
                    ins = dve.tensor_scalar(dst[:, b, :], src[:, b, :], mv[:, b, 0:1], rstd[:, b:b + 1],
                                            ALU.subtract, ALU.mult)
                if last_inc is None:
                    link(ins, base)
                else:
                    ins.then_inc(last_inc, 1)

            dve.memset(minus2[:, :], -2.0).then_inc(const_ok, 1)
            dve.memset(carrier[:, :], 0.0).then_inc(const_ok, 1)
            dve.wait_ge(const_ok, CONSTS)
            dve.wait_ge(x_in, 16)
            dve.wait_ge(weights_in, W_DMAS * 16)

            dve.sem_inc(misc_read, 1)
            SETUP_STEPS = 4 + 4 * RSQRT_STEPS
            with dve.Fori(0, GROUPS) as g:
                base = g * SETUP_STEPS
                steps[0] = 0
                rows_norm(xs[:, bass.ds(g * TB, TB), :], y, base, ln_ready)
                dve.wait_ge(misc_full, g * SETUP_MISC + 1)
                dve.tensor_copy(yT[:, :], misc[:, :]).then_inc(misc_read, 1)
                dve.wait_ge(misc_full, g * SETUP_MISC + 2)
                for b in range(TB):
                    ins = dve.tensor_tensor(msg[:, bass.ds(g * TB + b, 1), :].rearrange("p a d -> p (a d)"),
                                            misc[:, b * D:(b + 1) * D], bg_bc[:, :], ALU.add)
                ins.then_inc(misc_read, 1)

            for c in range(3):
                for hb in range(2):
                    mask_half(0, c, hb)
            for hb in range(2):
                square_half(0, 0, hb)

            SETUP_ALL = GROUPS * SETUP_STEPS
            POST_STEPS = 2 * SETUP_STEPS + 1 + 9

            def group(g, last):
                base = SETUP_ALL + g * POST_STEPS
                steps[0] = 0
                for c in range(CHUNKS):
                    for hb in range(2):
                        if not (last and c + 1 >= CHUNKS):
                            square_half(g + (c + 1) // CHUNKS, (c + 1) % CHUNKS, hb)
                    for hb in range(2):
                        if not (last and c + 3 >= CHUNKS):
                            mask_half(g + (c + 3) // CHUNKS, (c + 3) % CHUNKS, hb)
                results = SETUP_MISC * GROUPS + g * MISC

                dve.wait_ge(added, (g + 1) * PPG + WSLOTS)
                dve.tensor_copy(accT[:, :], acc[:, :]).then_inc(accT_out, 1)
                dve.wait_ge(misc_full, results + 1)
                dve.tensor_tensor(x1[:, :, :], misc[:, :].rearrange("p (b d) -> p b d", b=TB),
                                  xs[:, bass.ds(g * TB, TB), :], ALU.add).then_inc(misc_read, 1)
                dve.wait_ge(misc_read, 1 + results + 1)
                rows_norm(x1, y, base, ln_ready)
                dve.wait_ge(misc_full, results + 2)
                dve.tensor_copy(yT[:, :], misc[:, :]).then_inc(misc_read, 1)

                dve.wait_ge(misc_full, results + 3)
                for b in range(TB):
                    ins = dve.tensor_tensor(logits[:, b, :], misc[:, b * E:(b + 1) * E], gb_bc[:, :], ALU.add)
                ins.then_inc(misc_read, 1)
                dve.wait_ge(misc_read, 1 + results + 3)
                plain_next()
                for b in range(TB):
                    ins = dve.max(top8[:, b, :], logits[:, b, :])
                link(ins, base, plain=True)
                for b in range(TB):
                    ins = dve.max_index(idx8[:, b, :], top8[:, b, :], logits[:, b, :])
                link(ins, base)
                dve.tensor_tensor(dv[:, :], top8[:, :, 1], top8[:, :, 0], ALU.subtract).then_inc(diff_ready, 1)
                link(dve.tensor_copy(idxf[:, :, :], idx8[:, :, 0:2]), base)
                dve.wait_ge(exp_ready, g + 1)
                link(dve.tensor_scalar(p1[:, :], ed[:, :], 1.0, None, ALU.add), base)
                link(dve.reciprocal(p1[:, :], p1[:, :]), base)
                link(dve.tensor_tensor(p2[:, :], ed[:, :], p1[:, :], ALU.mult), base)
                for b in range(TB):
                    dve.tensor_scalar(ga[:, b, :], iota_e[:, :], idxf[:, b, 0:1], p1[:, b:b + 1],
                                      ALU.is_equal, ALU.mult)
                    ins = dve.tensor_scalar(gates[:, b, :], iota_e[:, :], idxf[:, b, 1:2], p2[:, b:b + 1],
                                            ALU.is_equal, ALU.mult)
                link(ins, base)
                dve.tensor_tensor(gates[:, :, :], gates[:, :, :], ga[:, :, :], ALU.add).then_inc(ln_ready, 1)
                dve.wait_ge(misc_full, results + 4)
                dve.tensor_copy(gatesT[:, :], misc[0:E, :]).then_inc(misc_read, 1)
                dve.wait_ge(misc_full, results + 5)
                dve.tensor_tensor(y[:, :, :], y[:, :, :], misc[:, :].rearrange("p (b d) -> p b d", b=TB),
                                  ALU.add).then_inc(misc_read, 1)
                dve.wait_ge(misc_read, 1 + results + 5)

                def combine(e):
                    dve.wait_ge(y_full, g * E + e + 1 + 2)
                    dve.wait_ge(y_read, g * E + e + 2)
                    for b in range(TB):
                        ins = dve.scalar_tensor_tensor(out=y[:, b, :], in0=yp[e % 2][:, b * D:(b + 1) * D],
                                                       scalar=gates[:, b, e:e + 1], in1=y[:, b, :],
                                                       op0=ALU.mult, op1=ALU.add)
                    ins.then_inc(y_read, 1)

                for e in range(E):
                    dve.wait_ge(hid_full, g * E + e + 1)
                    dve.wait_ge(y_full, g * E + e + 1)
                    dve.tensor_scalar(h[:, e % 2, 1, :], tp[e % 2][:, ROWS:2 * ROWS], b1s[:, e, 1:2], 0.0,
                                      ALU.add, ALU.max).then_inc(hid_act1, 1)
                    if e:
                        combine(e - 1)
                combine(E - 1)
                dve.wait_ge(y_read, (g + 1) * E + 2)

                rows_norm(y, y, base)
                def wide(t):
                    return t[:, :].unsqueeze(1).to_broadcast([P, TB, D])
                link(dve.tensor_tensor(y[:, :, :], y[:, :, :], wide(gamma_bc), ALU.mult), base)
                link(dve.tensor_tensor(y[:, :, :], y[:, :, :], wide(beta_bc), ALU.add), base)
                dve.wait_ge(fin_free, g + 1)
                dve.tensor_tensor(fin[:, :, :], y[:, :, :], x1[:, :, :], ALU.add).then_inc(fin_ready, 1)
                assert steps[0] == POST_STEPS

            dve.sem_inc(y_read, 2)
            with dve.Fori(0, GROUPS - 1) as g:
                group(g, False)
            group(GROUPS - 1, True)

        @block.tensor
        def _(pe):
            pe.sem_inc(added, WSLOTS)
            pe.sem_inc(y_full, 2)
            pe.wait_ge(const_ok, CONSTS)
            pe.wait_ge(weights_in, W_DMAS * 16)

            def turn_rows(src):
                for b in range(TB):
                    ins = pe.transpose(misc[0:src.shape[2], b * P:(b + 1) * P], src[:, b, :], ident[:, :])
                ins.then_inc(misc_full, 1)

            with pe.Fori(0, GROUPS) as g:
                pe.wait_ge(ln_ready, g + 1)
                turn_rows(y)
                pe.wait_ge(misc_read, 1 + g * SETUP_MISC + 1)
                for b in range(TB):
                    ins = pe.matmul(misc[:, b * D:(b + 1) * D], yT[:, b * P:(b + 1) * P], wgs[:, :],
                                    start=True, stop=True)
                ins.then_inc(misc_full, 1)
                pe.wait_ge(misc_read, 1 + g * SETUP_MISC + 2)

            def group(g, last):
                def products(m):
                    pe.wait_ge(weighted, g * PPG + m + 1 + 2)
                    for k in range(2):
                        n = 2 * m + k
                        ins = pe.matmul(acc[:, :], msg[:, n, :], wT[:, m % WSLOTS, k * ROWS:(k + 1) * ROWS],
                                        start=(n == 0), stop=(n == 2 * PPG - 1))
                    ins.then_inc(added, 1)

                for m in range(PPG):
                    c, k = divmod(m, PAIRS)
                    if k == 0:
                        pe.wait_ge(squared, (g * CHUNKS + c + 1) * 2)
                    pe.wait_ge(weighted, g * PPG + m + 1)
                    for t in range(2):
                        for b in range(TB):
                            j = (2 * k + t) * P
                            ins = pe.transpose(tp[m % 2][:, t * ROWS + b * P:t * ROWS + (b + 1) * P],
                                               chunk[:, c % RING, b, j:j + P], ident[:, :])
                    ins.then_inc(turned, 1)
                    if m:
                        products(m - 1)
                products(PPG - 1)

                results = 1 + SETUP_MISC * GROUPS + g * MISC
                pe.wait_ge(misc_read, results)
                pe.wait_ge(accT_out, g + 1)
                for b in range(TB):
                    ins = pe.transpose(misc[:, b * P:(b + 1) * P], accT[:, b * P:(b + 1) * P], ident[:, :])
                ins.then_inc(misc_full, 1)
                pe.wait_ge(ln_ready, GROUPS + 2 * g + 1)
                turn_rows(y)
                pe.wait_ge(misc_read, results + 2)
                for b in range(TB):
                    ins = pe.matmul(misc[:, b * E:(b + 1) * E], yT[:, b * P:(b + 1) * P], gws[:, :],
                                    start=True, stop=True)
                ins.then_inc(misc_full, 1)

                def hidden(e):
                    for t in range(FT):
                        ins = pe.matmul(tp[e % 2][:, t * ROWS:(t + 1) * ROWS], w1s[:, e, t * P:(t + 1) * P],
                                        yT[:, :], start=True, stop=True)
                    ins.then_inc(hid_full, 1)

                def output(e):
                    pe.wait_ge(hid_act0, g * E + e + 1)
                    pe.wait_ge(hid_act1, g * E + e + 1)
                    pe.wait_ge(y_read, g * E + e + 1)
                    for b in range(TB):
                        for t in range(FT):
                            ins = pe.matmul(yp[e % 2][:, b * D:(b + 1) * D], h[:, e % 2, t, b * P:(b + 1) * P],
                                            w2s[:, e, t, :], start=(t == 0), stop=(t == FT - 1))
                    ins.then_inc(y_full, 1)

                hidden(0)
                pe.wait_ge(ln_ready, GROUPS + 2 * g + 2)
                turn_rows(gates)
                pe.wait_ge(misc_read, results + 4)
                for b in range(TB):
                    ins = pe.matmul(misc[:, b * D:(b + 1) * D], gatesT[:, b * P:(b + 1) * P], b2s[:, :],
                                    start=True, stop=True)
                ins.then_inc(misc_full, 1)
                for e in range(1, E):
                    hidden(e)
                    output(e - 1)
                output(E - 1)

            with pe.Fori(0, GROUPS - 1) as g:
                group(g, False)
            group(GROUPS - 1, True)


_INS = ['x', 'adj', 'L0_gnn_W', 'L0_gnn_B', 'L0_ffn_gate_w', 'L0_ffn_gate_b', 'L0_ffn_w1', 'L0_ffn_b1',
        'L0_ffn_w2', 'L0_ffn_b2', 'L0_ffn_gamma', 'L0_ffn_beta']
_OUTS = [((8192, 128), 'float32')]


def kernel(**inputs):
    import numpy as _np
    import concourse.bacc as _bacc
    from concourse import mybir as _mybir
    from concourse.bass_utils import run_bass_kernel_spmd as _run

    nc = _bacc.Bacc("TRN2", target_bir_lowering=False, num_devices=1)
    arrays, args = {}, []
    for name in _INS:
        a = _np.ascontiguousarray(inputs[name])
        arrays[f"in_{name}_dram"] = a
        args.append(nc.dram_tensor(f"in_{name}_dram", a.shape, _mybir.dt.from_np(a.dtype), kind="ExternalInput").ap())
    for i, (shape, dtype) in enumerate(_OUTS):
        dt = _mybir.dt.from_np(_np.dtype(dtype))
        args.append(nc.dram_tensor(f"out_{i}_dram", shape, dt, kind="ExternalOutput").ap())
    gnn_moe_kernel(nc, *args)
    r = _run(nc, [arrays], core_ids=[0])
    got = tuple(r.results[0][f"out_{i}_dram"] for i in range(len(_OUTS)))
    return got[0]
```

```python
import concourse.bass as bass
from concourse import mybir
from contextlib import ExitStack

F32 = mybir.dt.float32
I32 = mybir.dt.int32
U32 = mybir.dt.uint32
ALU = mybir.AluOpType
ACT = mybir.ActivationFunctionType
AX = mybir.AxisListType

P = 128
EPS = 1e-5
TINY = 1e-18
RSQRT_BITS = 1597463007.0
RSQRT_STEPS = 3


def gnn_moe_kernel(nc, x, adj, gnn_w, gnn_b, gate_w, gate_b, w1, b1, w2, b2, gamma, beta, out):
    N, D = x.shape
    E, _, F = w1.shape
    FT = F // P
    K = 2
    TB = 4
    ROWS = TB * P
    GROUPS = N // ROWS
    JC = 1024
    CHUNKS = N // JC
    RING = 4
    PAIRS = JC // (2 * P)
    PPG = CHUNKS * PAIRS
    WSLOTS = 2
    HALF = TB // 2
    REGION = N + P
    TILES = K * N // P + E
    SPARE = E * REGION
    U = 4
    assert TILES % U == 0

    adj_v = adj.rearrange("(g b p) j -> p g b j", b=TB, p=P)
    out_v = out.rearrange("(g b p) d -> p g b d", b=TB, p=P)
    x_v = x.rearrange("(t p) d -> p t d", p=P)

    H = U // 2
    TURNS = TILES // U
    rows_in = nc.dram_tensor("rows_in", [SPARE + E * P, D], F32).ap()
    rows_out = nc.dram_tensor("rows_out", [TILES * P, D], F32).ap()
    results_v = rows_out.rearrange("(n u p) d -> p n u d", u=H, p=P)

    ctx = ExitStack()
    with ctx:
        def sb(name, shape, dt=F32):
            return ctx.enter_context(nc.sbuf_tensor(name, shape, dt))

        def sem(name):
            return ctx.enter_context(nc.semaphore(name))

        chunk = sb("chunk", [P, RING, TB, JC])
        wT = sb("wT", [P, WSLOTS, 2 * ROWS])
        msg = sb("msg", [P, N // P, D])
        xs = sb("xs", [P, N // P, D])
        w1s = sb("w1s", [P, E, F])
        w2s = sb("w2s", [P, FT, E, D])
        b1_bc = sb("b1_bc", [P, E, F])
        b2_bc = sb("b2_bc", [P, E, D])
        gws = sb("gws", [P, E])
        wgs = sb("wgs", [P, D])
        bg_bc = sb("bg_bc", [P, D])
        gb_bc = sb("gb_bc", [P, E])
        gamma_bc = sb("gamma_bc", [P, D])
        beta_bc = sb("beta_bc", [P, D])
        ident = sb("ident", [P, P])
        ones = sb("ones", [P, P])
        before = sb("before", [P, P])
        tiny = sb("tiny", [P, 1])
        minus2 = sb("minus2", [P, 1])
        zeros = sb("zeros", [P, D])
        pool_carrier = sb("pool_carrier", [1, 3])
        carrier = sb("carrier", [1, 2])
        iota_e = sb("iota_e", [P, E])
        region0 = sb("region0", [P, E])
        y = sb("y", [P, TB, D])
        yT = sb("yT", [P, ROWS])
        accT = yT
        stats = sb("stats", [P, TB, 6])
        mv = sb("mv", [P, N // P, 2])
        rstd = sb("rstd", [P, N // P])
        var = sb("var", [P, TB])
        nt = sb("nt", [P, TB])
        rs = sb("rs", [P, TB])
        logits = sb("logits", [P, TB, E])
        top8 = sb("top8", [P, TB, 8])
        idx8 = sb("idx8", [P, TB, 8], U32)
        idxf = sb("idxf", [P, TB, K])
        dv = sb("dv", [P, TB])
        ed = sb("ed", [P, TB])
        share = sb("share", [P, N // P, K])
        hot = sb("hot", [P, K, TB, E])
        both = sb("both", [P, TB, E])
        rank = sb("rank", [P, TB, E])
        picked = sb("picked", [P, K, TB, E])
        rowf = sb("rowf", [P, K, TB])
        row_now = sb("row_now", [P, K, TB], I32)
        row_all = sb("row_all", [P, GROUPS, K * TB])
        nexts = sb("nexts", [P, E])
        ends = sb("ends", [1, E], I32)
        count = sb("count", [P, E])
        tiles_of = sb("tiles_of", [P, E])
        tiles_to = [sb(f"tiles_to{i}", [P, E]) for i in range(2)]
        steps128 = sb("steps128", [P, N // P])
        tile_no = sb("tile_no", [1, TILES])
        mv_now = sb("mv_now", [P, TB, 2])
        w_tab = sb("w_tab", [1, H + TILES + U], I32)
        r_tab = sb("r_tab", [1, TILES], I32)
        ring = chunk[:, :, :, :].rearrange("p r b j -> p (r b j)")
        rin = ring[:, 0:U * D].rearrange("p (u d) -> p u d", u=U)
        rT = ring[:, 512:512 + U * P].rearrange("p (u d) -> p u d", u=U)
        hs = ring[:, 1024:1024 + U * F].rearrange("p (u f) -> p u f", u=U)
        hT = ring[:, 2048:2048 + U * F].rearrange("p (u f) -> p u f", u=U)
        ro = ring[:, 3072:3072 + U * D].rearrange("p (u d) -> p u d", u=U)
        back = [ring[:, 4096 + i * 1024:5120 + i * 1024].rearrange("p (k d) -> p k d", k=K * TB) for i in range(2)]
        zs = [ring[:, i:i + ROWS].rearrange("p (b d) -> p b d", b=TB) for i in (6144, 8192)]
        fin = [ring[:, 6656 + i * ROWS:6656 + (i + 1) * ROWS].rearrange("p (b d) -> p b d", b=TB) for i in range(2)]
        row_back = [ring[:, 7680 + i * K * TB:7680 + (i + 1) * K * TB].bitcast(I32) for i in range(2)]
        moved = ring[:, 13312:13312 + GROUPS * K * TB * (E - 1)].rearrange("p (r e) -> p r e", e=E - 1)
        move = ring[:, 15360:15360 + GROUPS * K * TB]
        many = ring[0:1, 8192:8192 + TILES * E].rearrange("p (t e) -> p t e", e=E)
        tile_e = ring[0:1, 11264:11264 + TILES]
        tile_s = ring[0:1, 11456:11456 + TILES]
        over = ring[:, 12288:12288 + E * (N // P)].rearrange("p (e k) -> p e k", e=E)

        tp = [ctx.enter_context(nc.psum_tensor(f"tp{i}", [P, 2 * ROWS], F32)) for i in range(2)]
        acc = ctx.enter_context(nc.psum_tensor("acc", [P, ROWS], F32))
        sp_ = [ctx.enter_context(nc.psum_tensor(f"spare{i}", [P, ROWS], F32)) for i in range(2)]
        misc = ctx.enter_context(nc.psum_tensor("misc", [P, ROWS], F32))
        bank_x = [tp[0][:, 0:ROWS], tp[1][:, 0:ROWS], acc[:, :], sp_[0][:, :]]
        bank_y = [tp[0][:, ROWS:2 * ROWS], tp[1][:, ROWS:2 * ROWS], misc[:, :], sp_[1][:, :]]

        loaded = [sem(f"chunk_loaded{i}") for i in range(RING)]
        weights_in = sem("weights_in")
        x_in = sem("x_in")
        masked = sem("masked")
        logged = sem("logged")
        inverted = sem("inverted")
        squared = sem("squared")
        turned = sem("turned")
        weighted = sem("weighted")
        added = sem("added")
        accT_out = sem("accT_out")
        blank = sem("blank")
        zeros_ok = sem("zeros_ok")
        const_ok = sem("const_ok")
        vec = sem("vector_step")
        ln_ready = sem("ln_ready")
        misc_full = sem("misc_full")
        misc_read = sem("misc_read")
        hot_ready = sem("hot_ready")
        diff_ready = sem("diff_ready")
        exp_ready = sem("exp_ready")
        rows_ready = sem("rows_ready")
        carried = sem("carried")
        scattered = sem("scattered")
        y_free = sem("y_free")
        table_ready = sem("table_ready")
        spare_zero = sem("spare_zero")
        padded = sem("padded")
        all_in = sem("all_in")
        rin_full = [sem(f"rin_full{u}") for u in range(U)]
        rin_turned = sem("rin_turned")
        rT_ready = sem("rT_ready")
        hid_full = sem("hid_full")
        hs_ready = sem("hs_ready")
        hid_turned = sem("hid_turned")
        hT_ready = sem("hT_ready")
        o_full = sem("o_full")
        ro_ready = sem("ro_ready")
        ro_out = [sem(f"ro_out{h}") for h in range(2)]
        idx_ready = sem("idx_ready")
        back_in = [sem(f"back_in{i}") for i in range(2)]
        fin_ready = sem("fin_ready")
        fin_free = sem("fin_free")
        stored = [sem(f"stored{i}") for i in range(2)]

        block = ctx.enter_context(nc.Block())

        W_DMAS = 9
        POOL_CONSTS = 8
        CONSTS = POOL_CONSTS + 3
        MISC = 4
        SETUP_MISC = 2

        def row(t):
            return t.rearrange("(a d) -> a d", a=1).partition_broadcast(P)

        def tile_experts(n, engine):
            _, values = nc.values_load_multi_w_load_instructions(
                w_tab[0:1, bass.ds(n * U, H + U)], engines=[engine], min_val=0, max_val=E - 1)
            return values

        @block.sync
        def _(sp):
            sp.dma_start(xs[:, :, :], x_v).then_inc(x_in, 16)

            def load(g, c):
                sp.dma_start(chunk[:, c % RING, :, :],
                             adj_v[:, g, :, c * JC:(c + 1) * JC]).then_inc(loaded[c % RING], 16)

            sp.dma_start(wgs[:, :], gnn_w).then_inc(x_in, 16)
            sp.dma_start(bg_bc[:, :], row(gnn_b)).then_inc(x_in, 16)
            for c in range(RING):
                load(0, c)
            for dst, src in ((gws[:, :], gate_w),
                             (gb_bc[:, :], row(gate_b)),
                             (w1s[:, :, :], w1.rearrange("e h f -> h e f")),
                             (w2s[:, 0, :, :], w2[:, 0:P, :].rearrange("e f h -> f e h")),
                             (w2s[:, 1, :, :], w2[:, P:2 * P, :].rearrange("e f h -> f e h")),
                             (b1_bc[:, :, :].rearrange("p e f -> p (e f)"), row(b1.rearrange("e f -> (e f)"))),
                             (b2_bc[:, :, :].rearrange("p e d -> p (e d)"), row(b2.rearrange("e d -> (e d)"))),
                             (gamma_bc[:, :], row(gamma)),
                             (beta_bc[:, :], row(beta))):
                sp.dma_start(dst, src).then_inc(weights_in, 16)

            def group(g, last):
                for c in range(CHUNKS):
                    if last and c + RING >= CHUNKS:
                        break
                    sp.wait_ge(turned, (g * CHUNKS + c + 1) * PAIRS)
                    n = c + RING
                    load(g + n // CHUNKS, n % CHUNKS)

            with sp.Fori(0, GROUPS - 1) as g:
                group(g, False)
            group(GROUPS - 1, True)

            sp.wait_ge(table_ready, 1)
            sp.wait_ge(all_in, 1)
            with sp.Fori(0, TILES // U) as n:
                for u in range(U):
                    r = sp.value_load(r_tab[0:1, bass.ds(n * U + u, 1)], min_val=0, max_val=SPARE + (E - 1) * P)
                    sp.wait_ge(rin_turned, n * U + u + 1)
                    sp.dma_start(rin[:, u, :], rows_in[bass.ds(r, P), :]).then_inc(rin_full[u], 16)

            sp.sem_inc(fin_free, 2)
            with sp.Fori(0, GROUPS // 2) as n:
                for i in range(2):
                    sp.wait_ge(fin_ready, 2 * n + i + 1)
                    sp.dma_start(out_v[:, 2 * n + i, :, :], fin[i]).then_inc(stored[i], 16)
                for i in range(2):
                    sp.wait_ge(stored[i], (n + 1) * 16)
                    sp.sem_inc(fin_free, 1)
            for i in range(2):
                sp.wait_ge(stored[i], GROUPS // 2 * 16)

        @block.gpsimd
        def _(pool):
            pool.memset(ident[:, :], 0.0).then_inc(blank, 1)
            pool.memset(before[:, :], 1.0).then_inc(blank, 1)
            pool.memset(ones[:, :], 1.0).then_inc(const_ok, 1)
            pool.memset(tiny[:, :], TINY).then_inc(const_ok, 1)
            pool.memset(zeros[:, :], 0.0).then_inc(zeros_ok, 1)
            pool.memset(pool_carrier[:, :], 0.0).then_inc(zeros_ok, 1)
            pool.iota(iota_e[:, :], pattern=[[1, E]], base=0, channel_multiplier=0,
                      allow_small_or_imprecise_dtypes=True).then_inc(const_ok, 1)
            pool.iota(region0[:, :], pattern=[[REGION, E]], base=0, channel_multiplier=0,
                      allow_small_or_imprecise_dtypes=True).then_inc(const_ok, 1)
            pool.iota(steps128[:, :], pattern=[[P, N // P]], base=0, channel_multiplier=0,
                      allow_small_or_imprecise_dtypes=True).then_inc(const_ok, 1)
            pool.iota(tile_no[:, :], pattern=[[1, TILES]], base=0, channel_multiplier=0,
                      allow_small_or_imprecise_dtypes=True).then_inc(const_ok, 1)
            pool.wait_ge(blank, 2)
            pool.affine_select(out=ident[:, :], in_=ident[:, :], compare_op=ALU.not_equal, fill=1.0,
                               base=0, pattern=[[-1, P]], channel_multiplier=1).then_inc(const_ok, 1)
            pool.affine_select(out=before[:, :], in_=before[:, :], compare_op=ALU.is_gt, fill=0.0,
                               base=0, pattern=[[1, P]], channel_multiplier=-1).then_inc(const_ok, 1)
            pool.wait_ge(zeros_ok, 2)
            for e in range(E):
                pool.dma_start(rows_in[SPARE + e * P:SPARE + (e + 1) * P, :], zeros[:, :]).then_inc(spare_zero, 16)

            def carry():
                pool.tensor_tensor(pool_carrier[0:1, 0:1], pool_carrier[0:1, 1:2], pool_carrier[0:1, 2:3],
                                   ALU.mult).then_inc(carried, 1)

            pool.sem_inc(y_free, 1)
            pool.sem_inc(carried, 1)
            with pool.Fori(0, GROUPS) as g:
                pool.wait_ge(carried, g + 1)
                pool.wait_ge(rows_ready, g + 1)
                carry()
                for k in range(K):
                    for b in range(TB):
                        pool.indirect_dma_start(
                            rows_in, bass.IndirectOffsetOnAxis(row_now[:, k, b:b + 1].bitcast(U32), 0),
                            y[:, b, :], None).then_inc(scattered, 16)
                pool.wait_ge(scattered, (g + 1) * K * TB * 16)
                pool.sem_inc(y_free, 1)

            pool.wait_ge(table_ready, 1)
            with pool.Fori(0, E) as e:
                end = pool.value_load(ends[0:1, bass.ds(e, 1)], min_val=0, max_val=SPARE - P)
                pool.dma_start(rows_in[bass.ds(end, P), :], zeros[:, :]).then_inc(padded, 16)
            pool.wait_ge(padded, E * 16)
            pool.wait_ge(spare_zero, E * 16)
            pool.sem_inc(all_in, 1)

            with pool.Fori(0, TURNS) as n:
                for h in range(2):
                    pool.wait_ge(ro_ready, n * U + (h + 1) * H)
                    pool.dma_start(results_v[:, bass.ds(2 * n + h, 1), :, :].rearrange("p a u d -> p (a u) d"),
                                   ro[:, h * H:(h + 1) * H, :]).then_inc(ro_out[h], 16)

            with pool.Fori(0, GROUPS // 2) as n:
                for i in range(2):
                    pool.wait_ge(carried, GROUPS + 2 * n + i + 1)
                    pool.wait_ge(idx_ready, 2 * n + i + 1)
                    carry()
                    for kb in range(K * TB):
                        pool.indirect_dma_start(
                            back[i][:, kb, :], None, rows_out,
                            bass.IndirectOffsetOnAxis(row_back[i][:, kb:kb + 1].bitcast(U32), 0)).then_inc(back_in[i], 16)

        @block.scalar
        def _(act):
            act.preload_act_table_set("natural_log_exp_and_others")
            act.sem_inc(weighted, 2)
            act.wait_ge(const_ok, CONSTS)

            def half(c, hb):
                return chunk[:, c % RING, hb * HALF:(hb + 1) * HALF, :]

            def log_half(g, c, hb):
                act.wait_ge(masked, (g * CHUNKS + c) * 2 + hb + 1)
                act.activation(half(c, hb), half(c, hb), ACT.Ln, bias=tiny[:, 0:1]).then_inc(logged, 1)

            def invert_half(g, c, hb):
                act.wait_ge(logged, (g * CHUNKS + c) * 2 + hb + 1)
                act.activation(half(c, hb), half(c, hb), ACT.Exp, scale=-1.0).then_inc(inverted, 1)

            def weigh(g, m):
                act.wait_ge(turned, g * PPG + m + 1)
                act.wait_ge(added, g * PPG + m + 1)
                act.activation(wT[:, m % WSLOTS, :], tp[m % 2][:, :], ACT.Exp, bias=minus2[:, 0:1],
                               scale=-2.0).then_inc(weighted, 1)

            def soften(g):
                act.wait_ge(diff_ready, g + 1)
                act.activation(ed[:, :], dv[:, :], ACT.Exp).then_inc(exp_ready, 1)

            def group(g, gate, last):
                for m in range(PPG):
                    c, k = divmod(m, PAIRS)
                    weigh(g, m)
                    n = c + 2
                    if not (last and n >= CHUNKS):
                        (log_half if k < 2 else invert_half)(g + n // CHUNKS, n % CHUNKS, k % 2)
                    if gate and m == 9:
                        soften(g - 1)

            for c in range(2):
                for hb in range(2):
                    log_half(0, c, hb)
                for hb in range(2):
                    invert_half(0, c, hb)
            group(0, False, False)
            with act.Fori(1, GROUPS - 1) as g:
                group(g, True, False)
            group(GROUPS - 1, True, True)
            soften(GROUPS - 1)

            def copy_rows(n, h):
                for i in range(H):
                    u = (h % 2) * H + i
                    act.wait_ge(rin_turned, U + n * U + h * H + i + 1)
                    act.activation(rT[:, u, :], bank_x[u][:, 0:P], ACT.Copy).then_inc(rT_ready, 1)

            def relu_hidden(n, h):
                for i in range(H):
                    u = (h % 2) * H + i
                    act.wait_ge(hid_turned, n * U + h * H + i + 1)
                    act.activation(hT[:, u, :], bank_x[u][:, P:P + F], ACT.Relu).then_inc(hT_ready, 1)

            def step(n, last):
                copy_rows(n, 1)
                relu_hidden(n, 0)
                if not last:
                    copy_rows(n, 2)
                relu_hidden(n, 1)

            copy_rows(0, 0)
            with act.Fori(0, TURNS - 1) as n:
                step(n, False)
            step(TURNS - 1, True)

        @block.vector
        def _(dve):
            steps = [0]

            def plain_next():
                dve.tensor_copy(carrier[0:1, 1:2], carrier[0:1, 0:1])

            def link(ins, base, plain=False):
                steps[0] += 1
                ins.then_inc(vec, 1)
                dve.wait_ge(vec, base + steps[0])
                if plain:
                    plain_next()

            def half(c, hb):
                return chunk[:, c % RING, hb * HALF:(hb + 1) * HALF, :]

            def mask_half(g, c, hb):
                if hb == 0:
                    dve.wait_ge(loaded[c % RING], (g * (CHUNKS // RING) + c // RING + 1) * 16)
                dve.scalar_tensor_tensor(out=half(c, hb), in0=half(c, hb), scalar=1.0, in1=half(c, hb),
                                         op0=ALU.is_lt, op1=ALU.mult).then_inc(masked, 1)

            def square_half(g, c, hb):
                dve.wait_ge(inverted, (g * CHUNKS + c) * 2 + hb + 1)
                dve.scalar_tensor_tensor(out=half(c, hb), in0=half(c, hb), scalar=2.0, in1=half(c, hb),
                                         op0=ALU.subtract, op1=ALU.mult).then_inc(squared, 1)

            def rows_norm(src, dst, base, last_inc=None):
                plain_next()
                for b in range(TB):
                    ins = dve.bn_stats(stats[:, b, :], src[:, b, :])
                link(ins, base, plain=True)
                for b in range(TB):
                    ins = dve.bn_aggr(mv_now[:, b, :], stats[:, b, :])
                link(ins, base)
                link(dve.tensor_scalar(var[:, :], mv_now[:, :, 1], EPS, None, ALU.add), base)
                link(dve.tensor_scalar(rs[:, :].bitcast(I32), var[:, :].bitcast(I32), -0.5, RSQRT_BITS,
                                       ALU.mult, ALU.add), base)
                for _ in range(RSQRT_STEPS):
                    link(dve.tensor_tensor(nt[:, :], rs[:, :], rs[:, :], ALU.mult), base)
                    link(dve.tensor_tensor(nt[:, :], nt[:, :], var[:, :], ALU.mult), base)
                    link(dve.tensor_scalar(nt[:, :], nt[:, :], -0.5, 1.5, ALU.mult, ALU.add), base)
                    link(dve.tensor_tensor(rs[:, :], rs[:, :], nt[:, :], ALU.mult), base)
                ins = normalise(src, dst, mv_now, rs)
                if last_inc is None:
                    link(ins, base)
                else:
                    ins.then_inc(last_inc, 1)

            def normalise(src, dst, mvs, rss):
                for b in range(TB):
                    ins = dve.tensor_scalar(dst[:, b, :], src[:, b, :], mvs[:, b, 0:1], rss[:, b:b + 1],
                                            ALU.subtract, ALU.mult)
                return ins

            def blocks(t, g):
                return t[:, bass.ds(g * TB, TB), :] if len(t.shape) == 3 else t[:, bass.ds(g * TB, TB)]

            dve.memset(w_tab[:, :], 0).then_inc(const_ok, 1)
            dve.memset(minus2[:, :], -2.0).then_inc(const_ok, 1)
            dve.memset(carrier[:, :], 0.0).then_inc(const_ok, 1)
            dve.wait_ge(const_ok, CONSTS)
            for hb in range(2):
                mask_half(0, 0, hb)

            dve.sem_inc(misc_read, 1)
            dve.wait_ge(x_in, 3 * 16)
            NORM_STEPS = 4 + 4 * RSQRT_STEPS
            def norm_group(g):
                steps[0] = 0
                rows_norm(blocks(xs, g), y, g * NORM_STEPS, ln_ready)

            def keep_group(g, more):
                dve.wait_ge(misc_full, g * SETUP_MISC + 1)
                dve.tensor_copy(yT[:, :], misc[:, :]).then_inc(misc_read, 1)
                if more:
                    norm_group(g + 1)
                dve.wait_ge(misc_full, g * SETUP_MISC + 2)
                dve.tensor_tensor(blocks(msg, g), misc[:, :].rearrange("p (b d) -> p b d", b=TB),
                                  bg_bc[:, :].unsqueeze(1).to_broadcast([P, TB, D]), ALU.add).then_inc(misc_read, 1)

            norm_group(0)
            with dve.Fori(0, GROUPS - 1) as g:
                keep_group(g, True)
            keep_group(GROUPS - 1, False)

            for c in range(1, 3):
                for hb in range(2):
                    mask_half(0, c, hb)
            for hb in range(2):
                square_half(0, 0, hb)
            dve.wait_ge(weights_in, W_DMAS * 16)
            SETUP_ALL = GROUPS * NORM_STEPS
            GATE_STEPS = 10
            dve.tensor_copy(nexts[:, :], region0[:, :]).then_inc(vec, 1)
            dve.wait_ge(vec, SETUP_ALL + 1)

            def spread(t, shape):
                return t.to_broadcast(shape)

            def gate_sum(g):
                dve.wait_ge(added, (g + 1) * PPG + WSLOTS)
                dve.tensor_copy(accT[:, :], acc[:, :]).then_inc(accT_out, 1)

            def gate_base(g):
                return SETUP_ALL + 1 + g * (NORM_STEPS + GATE_STEPS)

            def gate_rows(g):
                base = gate_base(g)
                steps[0] = 0
                dve.wait_ge(misc_full, SETUP_MISC * GROUPS + g * MISC + 1)
                dve.tensor_tensor(blocks(xs, g), misc[:, :].rearrange("p (b d) -> p b d", b=TB),
                                  blocks(xs, g), ALU.add).then_inc(misc_read, 1)
                dve.wait_ge(misc_read, 1 + SETUP_MISC * GROUPS + g * MISC + 1)
                dve.wait_ge(y_free, g + 1)
                rows_norm(blocks(xs, g), y, base, ln_ready)
                dve.tensor_copy(blocks(mv, g), mv_now[:, :, :])
                dve.tensor_copy(blocks(rstd, g), rs[:, :])

            def gate_turn(g):
                dve.wait_ge(misc_full, SETUP_MISC * GROUPS + g * MISC + 2)
                dve.tensor_copy(yT[:, :], misc[:, :]).then_inc(misc_read, 1)

            def gate_choose(g):
                base = gate_base(g)
                results = SETUP_MISC * GROUPS + g * MISC
                dve.wait_ge(misc_full, results + 3)
                dve.tensor_tensor(logits[:, :, :], misc[:, 0:TB * E].rearrange("p (b e) -> p b e", b=TB),
                                  gb_bc[:, :].unsqueeze(1).to_broadcast([P, TB, E]), ALU.add).then_inc(misc_read, 1)
                dve.wait_ge(misc_read, 1 + results + 3)
                plain_next()
                for b in range(TB):
                    ins = dve.max(top8[:, b, :], logits[:, b, :])
                link(ins, base, plain=True)
                for b in range(TB):
                    ins = dve.max_index(idx8[:, b, :], top8[:, b, :], logits[:, b, :])
                link(ins, base)
                dve.tensor_tensor(dv[:, :], top8[:, :, 1], top8[:, :, 0], ALU.subtract).then_inc(diff_ready, 1)
                link(dve.tensor_copy(idxf[:, :, :], idx8[:, :, 0:K]), base)
                for k in range(K):
                    ins = dve.tensor_tensor(hot[:, k, :, :], iota_e[:, :].unsqueeze(1).to_broadcast([P, TB, E]),
                                            idxf[:, :, k:k + 1].to_broadcast([P, TB, E]), ALU.is_equal)
                link(ins, base)
                dve.tensor_tensor(both[:, :, :], hot[:, 0, :, :], hot[:, 1, :, :], ALU.add).then_inc(hot_ready, 1)

            def gate_place(g):
                base = gate_base(g)
                dve.wait_ge(misc_full, SETUP_MISC * GROUPS + g * MISC + 4)
                dve.tensor_tensor(rank[:, :, :], misc[:, 0:TB * E].rearrange("p (b e) -> p b e", b=TB),
                                  nexts[:, :].unsqueeze(1).to_broadcast([P, TB, E]), ALU.add).then_inc(vec, 1)
                steps[0] += 1
                dve.wait_ge(vec, base + steps[0])
                dve.tensor_tensor(nexts[:, :], misc[:, TB * E:(TB + 1) * E], nexts[:, :], ALU.add).then_inc(misc_read, 1)
                link(dve.tensor_tensor(picked[:, :, :, :], hot[:, :, :, :],
                                       rank[:, :, :].unsqueeze(1).to_broadcast([P, K, TB, E]), ALU.mult), base)
                link(dve.reduce_sum(rowf[:, :, :], picked[:, :, :, :], AX.X), base)
                dve.tensor_copy(row_all[:, bass.ds(g, 1), :].rearrange("p a k -> p (a k)"),
                                rowf[:, :, :].rearrange("p k b -> p (k b)"))
                dve.tensor_copy(row_now[:, :, :], rowf[:, :, :]).then_inc(rows_ready, 1)
                dve.wait_ge(exp_ready, g + 1)
                link(dve.tensor_scalar(dv[:, :], ed[:, :], 1.0, None, ALU.add), base)
                link(dve.reciprocal(dv[:, :], dv[:, :]), base)
                mine = blocks(share, g)
                dve.tensor_copy(mine[:, :, 0], dv[:, :])
                link(dve.tensor_tensor(mine[:, :, 1], ed[:, :], dv[:, :], ALU.mult), base)

            def group(g, gate, last):
                if gate:
                    gate_sum(g - 1)
                for m in range(PPG):
                    c, k = divmod(m, PAIRS)
                    n = c + (1 if k < 2 else 3)
                    if not (last and n >= CHUNKS):
                        (square_half if k < 2 else mask_half)(g + n // CHUNKS, n % CHUNKS, k % 2)
                    if gate and m == 2:
                        gate_rows(g - 1)
                    if gate and m == 5:
                        gate_turn(g - 1)
                    if gate and m == 7:
                        gate_choose(g - 1)
                    if gate and m == 11:
                        gate_place(g - 1)
                        assert steps[0] == NORM_STEPS + GATE_STEPS

            group(0, False, False)
            with dve.Fori(1, GROUPS - 1) as g:
                group(g, True, False)
            group(GROUPS - 1, True, True)
            g = GROUPS - 1
            gate_sum(g)
            gate_rows(g)
            gate_turn(g)
            gate_choose(g)
            gate_place(g)

            base = gate_base(GROUPS)
            steps[0] = 0
            link(dve.tensor_copy(ends[:, :], nexts[0:1, :]), base)
            link(dve.tensor_tensor(count[:, :], nexts[:, :], region0[:, :], ALU.subtract), base)
            NB = N // P
            link(dve.tensor_tensor(over, count[:, :].unsqueeze(2).to_broadcast([P, E, NB]),
                                   steps128[:, :].unsqueeze(1).to_broadcast([P, E, NB]), ALU.is_gt), base)
            link(dve.reduce_sum(tiles_of[:, :], over, AX.X), base)
            upto, step = tiles_of, 1
            while step < E:
                to = tiles_to[0] if upto is not tiles_to[0] else tiles_to[1]
                dve.tensor_copy(to[:, 0:step], upto[:, 0:step])
                link(dve.tensor_tensor(to[:, step:E], upto[:, step:E], upto[:, 0:E - step], ALU.add), base)
                upto, step = to, 2 * step
            link(dve.tensor_tensor(many, upto[0:1, :].unsqueeze(1).to_broadcast([1, TILES, E]),
                                   tile_no[:, :].unsqueeze(2).to_broadcast([1, TILES, E]), ALU.is_le), base)
            link(dve.reduce_sum(tile_e, many, AX.X), base)
            link(dve.tensor_tensor(many, many, tiles_of[0:1, :].unsqueeze(1).to_broadcast([1, TILES, E]), ALU.mult), base)
            link(dve.reduce_sum(tile_s, many, AX.X), base)
            link(dve.tensor_tensor(tile_s, tile_no[:, :], tile_s, ALU.subtract), base)
            link(dve.tensor_scalar(w_tab[:, H:H + TILES], tile_e, float(E - 1), None, ALU.min), base)
            link(dve.tensor_scalar(tile_e, tile_e, float(REGION), None, ALU.mult), base)
            dve.scalar_tensor_tensor(out=r_tab[:, :], in0=tile_s, scalar=float(P), in1=tile_e,
                                     op0=ALU.mult, op1=ALU.add).then_inc(table_ready, 1)
            dve.wait_ge(table_ready, 1)
            link(dve.tensor_scalar(tiles_of[:, :], tiles_of[:, :], float(P), -float(REGION), ALU.mult, ALU.add), base)
            rows_flat = row_all[:, :, :].rearrange("p g k -> p (g k)")
            wide = [P, GROUPS * K * TB, E - 1]
            link(dve.tensor_tensor(moved, rows_flat.unsqueeze(2).to_broadcast(wide),
                                   region0[:, 1:E].unsqueeze(1).to_broadcast(wide), ALU.is_ge), base)
            link(dve.tensor_tensor(moved, moved, tiles_of[:, 0:E - 1].unsqueeze(1).to_broadcast(wide), ALU.mult), base)
            link(dve.reduce_sum(move, moved, AX.X), base)
            link(dve.tensor_tensor(rows_flat, rows_flat, move, ALU.add), base)

            def bias_hidden(n, h):
                for i in range(H):
                    u = (h % 2) * H + i
                    e = experts[h * H + i + H]
                    dve.wait_ge(hid_full, n * U + h * H + i + 1)
                    dve.tensor_tensor(hs[:, u, :], bank_y[u][:, P:P + F],
                                      b1_bc[:, bass.ds(e, 1), :].rearrange("p a f -> p (a f)"), ALU.add).then_inc(hs_ready, 1)

            def bias_output(n, h, first=False):
                for i in range(H):
                    u = (h % 2) * H + i
                    e = experts[h * H + i + H]
                    dve.wait_ge(o_full, n * U + h * H + i + 1)
                    if i == 0 and not first:
                        dve.wait_ge(ro_out[h % 2], (n + h) * 16)
                    dve.tensor_tensor(ro[:, u, :], bank_y[u][:, 0:D],
                                      b2_bc[:, bass.ds(e, 1), :].rearrange("p a d -> p (a d)"), ALU.add).then_inc(ro_ready, 1)

            experts = []

            def step(n, kind):
                experts[:] = tile_experts(n, mybir.EngineType.DVE)
                bias_hidden(n, 0)
                if kind != "first":
                    bias_output(n, -1, kind == "second")
                bias_hidden(n, 1)
                bias_output(n, 0, kind == "first")

            step(0, "first")
            step(1, "second")
            with dve.Fori(2, TURNS) as n:
                step(n, "middle")
            experts[:] = tile_experts(TURNS, mybir.EngineType.DVE)
            bias_output(TURNS, -1)

            for h in range(2):
                dve.wait_ge(ro_out[h], TURNS * 16)
            for i in range(2):
                dve.tensor_copy(row_back[i], row_all[:, i, :]).then_inc(idx_ready, 1)
            LIST_STEPS = steps[0]
            LAST_STEPS = NORM_STEPS + 6

            def last_stage(g, i, n, more):
                lbase = base + LIST_STEPS + g * LAST_STEPS
                steps[0] = 0
                z = zs[i]
                link(normalise(blocks(xs, g), z, blocks(mv, g), blocks(rstd, g)), lbase)
                dve.wait_ge(back_in[i], (n + 1) * K * TB * 16)
                mine = blocks(share, g)
                for k in range(K):
                    for b in range(TB):
                        ins = dve.scalar_tensor_tensor(out=z[:, b, :], in0=back[i][:, k * TB + b, :],
                                                       scalar=mine[:, b, k:k + 1], in1=z[:, b, :],
                                                       op0=ALU.mult, op1=ALU.add)
                    link(ins, lbase)
                if more:
                    dve.tensor_copy(row_back[i], row_all[:, bass.ds(g + 2, 1), :].rearrange("p a k -> p (a k)")).then_inc(idx_ready, 1)
                rows_norm(z, z, lbase)
                link(dve.tensor_tensor(z, z, gamma_bc[:, :].unsqueeze(1).to_broadcast([P, TB, D]), ALU.mult), lbase)
                link(dve.tensor_tensor(z, z, beta_bc[:, :].unsqueeze(1).to_broadcast([P, TB, D]), ALU.add), lbase)
                assert steps[0] == LAST_STEPS
                dve.wait_ge(fin_free, g + 1)
                dve.tensor_tensor(fin[i], z, blocks(xs, g), ALU.add).then_inc(fin_ready, 1)

            with dve.Fori(0, GROUPS // 2 - 1) as n:
                for i in range(2):
                    last_stage(2 * n + i, i, n, True)
            for i in range(2):
                last_stage(GROUPS - 2 + i, i, GROUPS // 2 - 1, False)

        @block.tensor
        def _(pe):
            pe.sem_inc(added, WSLOTS)
            pe.wait_ge(const_ok, CONSTS)
            pe.wait_ge(x_in, 3 * 16)

            def turn_rows():
                for b in range(TB):
                    ins = pe.transpose(misc[:, b * P:(b + 1) * P], y[:, b, :], ident[:, :])
                ins.then_inc(misc_full, 1)

            with pe.Fori(0, GROUPS) as g:
                pe.wait_ge(ln_ready, g + 1)
                turn_rows()
                pe.wait_ge(misc_read, 1 + g * SETUP_MISC + 1)
                for b in range(TB):
                    ins = pe.matmul(misc[:, b * D:(b + 1) * D], yT[:, b * P:(b + 1) * P], wgs[:, :],
                                    start=True, stop=True)
                ins.then_inc(misc_full, 1)
                pe.wait_ge(misc_read, 1 + g * SETUP_MISC + 2)

            def gate_sum(g):
                pe.wait_ge(misc_read, 1 + SETUP_MISC * GROUPS + g * MISC)
                for b in range(TB):
                    ins = pe.transpose(misc[:, b * P:(b + 1) * P], accT[:, b * P:(b + 1) * P], ident[:, :])
                ins.then_inc(misc_full, 1)

            def gate_turn(g):
                pe.wait_ge(ln_ready, GROUPS + g + 1)
                turn_rows()

            def gate_logits(g):
                pe.wait_ge(misc_read, 1 + SETUP_MISC * GROUPS + g * MISC + 2)
                for b in range(TB):
                    ins = pe.matmul(misc[:, b * E:(b + 1) * E], yT[:, b * P:(b + 1) * P], gws[:, :],
                                    start=True, stop=True)
                ins.then_inc(misc_full, 1)

            def gate_ranks(g):
                pe.wait_ge(hot_ready, g + 1)
                flat = both[:, :, :].rearrange("p b e -> p (b e)")
                pe.matmul(misc[:, 0:TB * E], before[:, :], flat, start=True, stop=False, skip_group_check=True)
                for d in range(1, TB):
                    pe.matmul(misc[:, d * E:TB * E], ones[:, :], flat[:, 0:(TB - d) * E], start=False,
                              stop=(d == TB - 1), skip_group_check=True)
                for b in range(TB):
                    ins = pe.matmul(misc[:, TB * E:(TB + 1) * E], ones[:, :], flat[:, b * E:(b + 1) * E],
                                    start=(b == 0), stop=(b == TB - 1), skip_group_check=True)
                ins.then_inc(misc_full, 1)

            def group(g, gate, last):
                def products(m):
                    pe.wait_ge(weighted, g * PPG + m + 1 + 2)
                    if gate and m == 0:
                        pe.wait_ge(accT_out, g)
                    for k in range(2):
                        n = 2 * m + k
                        ins = pe.matmul(acc[:, :], msg[:, n, :], wT[:, m % WSLOTS, k * ROWS:(k + 1) * ROWS],
                                        start=(n == 0), stop=(n == 2 * PPG - 1))
                    ins.then_inc(added, 1)

                for m in range(PPG):
                    c, k = divmod(m, PAIRS)
                    if k == 0:
                        pe.wait_ge(squared, (g * CHUNKS + c + 1) * 2)
                    pe.wait_ge(weighted, g * PPG + m + 1)
                    for t in range(2):
                        for b in range(TB):
                            j = (2 * k + t) * P
                            ins = pe.transpose(tp[m % 2][:, t * ROWS + b * P:t * ROWS + (b + 1) * P],
                                               chunk[:, c % RING, b, j:j + P], ident[:, :])
                    ins.then_inc(turned, 1)
                    if m:
                        products(m - 1)
                    if gate and m == 1:
                        gate_sum(g - 1)
                    if gate and m == 4:
                        gate_turn(g - 1)
                    if gate and m == 6:
                        gate_logits(g - 1)
                    if gate and m == 10:
                        gate_ranks(g - 1)
                products(PPG - 1)

            pe.wait_ge(weights_in, W_DMAS * 16)
            group(0, False, False)
            with pe.Fori(1, GROUPS - 1) as g:
                group(g, True, False)
            g = GROUPS - 1
            group(g, True, True)
            pe.wait_ge(accT_out, GROUPS)
            gate_sum(g)
            gate_turn(g)
            gate_logits(g)
            gate_ranks(g)

            pe.sem_inc(rin_turned, U)
            pe.wait_ge(misc_read, 1 + SETUP_MISC * GROUPS + GROUPS * MISC)
            pe.wait_ge(table_ready, 1)
            def turn_tile(n, h, first=False):
                for i in range(H):
                    u = (h % 2) * H + i
                    if not first:
                        pe.wait_ge(hT_ready, n * U + h * H + i + 1 - U)
                    pe.wait_ge(rin_full[u], (n + 1 + h // 2) * 16)
                    pe.transpose(bank_x[u][:, 0:P], rin[:, u, :], ident[:, :]).then_inc(rin_turned, 1)

            def hidden(n, h, first=False):
                for i in range(H):
                    u = (h % 2) * H + i
                    e = experts[h * H + i + H]
                    if not first:
                        pe.wait_ge(ro_ready, n * U + h * H + i + 1 - U)
                    pe.wait_ge(rT_ready, n * U + h * H + i + 1)
                    pe.matmul(bank_y[u][:, P:P + F], rT[:, u, :],
                              w1s[:, bass.ds(e, 1), :].rearrange("p a f -> p (a f)"),
                              start=True, stop=True).then_inc(hid_full, 1)

            def turn_hidden(n, h):
                for i in range(H):
                    u = (h % 2) * H + i
                    pe.wait_ge(hs_ready, n * U + h * H + i + 1)
                    for t in range(FT):
                        ins = pe.transpose(bank_x[u][:, P + t * P:P + (t + 1) * P], hs[:, u, t * P:(t + 1) * P],
                                           ident[:, :])
                    ins.then_inc(hid_turned, 1)

            def output(n, h):
                for i in range(H):
                    u = (h % 2) * H + i
                    e = experts[h * H + i + H]
                    pe.wait_ge(hT_ready, n * U + h * H + i + 1)
                    for t in range(FT):
                        ins = pe.matmul(bank_y[u][:, 0:D], hT[:, u, t * P:(t + 1) * P],
                                        w2s[:, t, bass.ds(e, 1), :].rearrange("p a d -> p (a d)"),
                                        start=(t == 0), stop=(t == FT - 1))
                    ins.then_inc(o_full, 1)

            experts = []

            def step(n, kind):
                experts[:] = tile_experts(n, mybir.EngineType.PE)
                hidden(n, 0, kind == "first")
                if kind != "first":
                    output(n, -1)
                turn_tile(n, 1, kind == "first")
                turn_hidden(n, 0)
                hidden(n, 1, kind == "first")
                output(n, 0)
                if kind != "last":
                    turn_tile(n, 2)
                turn_hidden(n, 1)

            turn_tile(0, 0, True)
            step(0, "first")
            with pe.Fori(1, TURNS - 1) as n:
                step(n, "middle")
            step(TURNS - 1, "last")
            experts[:] = tile_experts(TURNS, mybir.EngineType.PE)
            output(TURNS, -1)

_INS = ['x', 'adj', 'L0_gnn_W', 'L0_gnn_B', 'L0_ffn_gate_w', 'L0_ffn_gate_b', 'L0_ffn_w1', 'L0_ffn_b1',
        'L0_ffn_w2', 'L0_ffn_b2', 'L0_ffn_gamma', 'L0_ffn_beta']
_OUTS = [((8192, 128), 'float32')]


def kernel(**inputs):
    import numpy as _np
    import concourse.bacc as _bacc
    from concourse import mybir as _mybir
    from concourse.bass_utils import run_bass_kernel_spmd as _run

    nc = _bacc.Bacc("TRN2", target_bir_lowering=False, num_devices=1)
    arrays, args = {}, []
    for name in _INS:
        a = _np.ascontiguousarray(inputs[name])
        arrays[f"in_{name}_dram"] = a
        args.append(nc.dram_tensor(f"in_{name}_dram", a.shape, _mybir.dt.from_np(a.dtype), kind="ExternalInput").ap())
    for i, (shape, dtype) in enumerate(_OUTS):
        dt = _mybir.dt.from_np(_np.dtype(dtype))
        args.append(nc.dram_tensor(f"out_{i}_dram", shape, dt, kind="ExternalOutput").ap())
    gnn_moe_kernel(nc, *args)
    r = _run(nc, [arrays], core_ids=[0])
    got = tuple(r.results[0][f"out_{i}_dram"] for i in range(len(_OUTS)))
    return got[0]
```

```python
import concourse.bass as bass
from concourse import mybir
from contextlib import ExitStack

F32 = mybir.dt.float32
I32 = mybir.dt.int32
U32 = mybir.dt.uint32
ALU = mybir.AluOpType
ACT = mybir.ActivationFunctionType
AX = mybir.AxisListType

P = 128
EPS = 1e-5
TINY = 1e-18


def gnn_moe_kernel(nc, x, adj, gnn_w, gnn_b, gate_w, gate_b, w1, b1, w2, b2, gamma, beta, out):
    N, D = x.shape
    E, _, F = w1.shape
    FT = F // P
    K = 2
    TB = 4
    ROWS = TB * P
    GROUPS = N // ROWS
    JC = 512
    CHUNKS = N // JC
    RING = 8
    PAIRS = JC // (2 * P)
    PPG = CHUNKS * PAIRS
    WSLOTS = 2
    SQUARE_LEAD, LOG_LEAD, MASK_LEAD = 2, 4, 6
    assert PAIRS == 2 and CHUNKS % RING == 0 and RING % 2 == 0
    U = 4
    H = U // 2
    PR = H * P
    REGION = N + PR
    PACKS = K * N // PR + E
    TURNS = PACKS // 2
    assert PACKS % 2 == 0
    SPARE = E * REGION

    adj_v = adj.rearrange("(g b p) j -> p g b j", b=TB, p=P)
    out_v = out.rearrange("(g b p) d -> p g b d", b=TB, p=P)
    x_v = x.rearrange("(t p) d -> p t d", p=P)

    rows_in = nc.dram_tensor("rows_in", [SPARE + E * PR, D], F32).ap()
    rows_out = nc.dram_tensor("rows_out", [PACKS * PR, D], F32).ap()
    results_v = rows_out.rearrange("(n u p) d -> p n u d", u=H, p=P)

    ctx = ExitStack()
    with ctx:
        def sb(name, shape, dt=F32):
            return ctx.enter_context(nc.sbuf_tensor(name, shape, dt))

        def sem(name):
            return ctx.enter_context(nc.semaphore(name))

        chunk = sb("chunk", [P, RING, TB, JC])
        wT = sb("wT", [P, WSLOTS, 2 * ROWS])
        msg = sb("msg", [P, N // P, D])
        xs = sb("xs", [P, N // P, D])
        w1s = sb("w1s", [P, E, F])
        w2s = sb("w2s", [P, FT, E, D])
        b1_bc = sb("b1_bc", [P, E, F])
        b2_bc = sb("b2_bc", [P, E, D])
        gws = sb("gws", [P, E])
        wgs = sb("wgs", [P, D])
        bg_bc = sb("bg_bc", [P, D])
        gb_bc = sb("gb_bc", [P, E])
        gamma_bc = sb("gamma_bc", [P, D])
        beta_bc = sb("beta_bc", [P, D])
        ident = sb("ident", [P, P])
        ones = sb("ones", [P, P])
        before = sb("before", [P, P])
        tiny = sb("tiny", [P, 1])
        minus2 = sb("minus2", [P, 1])
        eps = sb("eps", [P, 1])
        zeros = sb("zeros", [P, H, D])
        pool_carrier = sb("pool_carrier", [1, 3])
        carrier = sb("carrier", [1, 2])
        iota_e = sb("iota_e", [P, E])
        region0 = sb("region0", [P, E])
        y = sb("y", [P, TB, D])
        yT = sb("yT", [P, ROWS])
        accT = yT
        stats = sb("stats", [P, TB, 6])
        mv = sb("mv", [P, N // P, 2])
        rstd = sb("rstd", [P, N // P])
        lnv = sb("lnv", [P, TB])
        nt = sb("nt", [P, TB])
        shift = sb("shift", [P, 2, TB])
        shift_all = sb("shift_all", [P, N // P])
        rs = sb("rs", [P, 2, TB])
        logits = sb("logits", [P, TB, E])
        top8 = sb("top8", [P, TB, 8])
        idx8 = sb("idx8", [P, TB, 8], U32)
        idxf = sb("idxf", [P, TB, K])
        dv = sb("dv", [P, TB])
        ed = sb("ed", [P, TB])
        share = sb("share", [P, N // P, K])
        hot = sb("hot", [P, K, TB, E])
        both = sb("both", [P, TB, E])
        rank = sb("rank", [P, TB, E])
        picked = sb("picked", [P, K, TB, E])
        rowf = sb("rowf", [P, K, TB])
        row_now = sb("row_now", [P, K, TB], I32)
        row_all = sb("row_all", [P, GROUPS, K * TB])
        nexts = sb("nexts", [P, E])
        ends = sb("ends", [1, E], I32)
        count = sb("count", [P, E])
        packs_of = sb("packs_of", [P, E])
        packs_to = [sb(f"packs_to{i}", [P, E]) for i in range(2)]
        pack_steps = sb("pack_steps", [P, N // PR])
        pack_no = sb("pack_no", [1, PACKS])
        mv_now = sb("mv_now", [P, 2, TB, 2])
        w_tab = sb("w_tab", [1, 1 + PACKS + 2], I32)
        r_tab = sb("r_tab", [1, PACKS], I32)
        ring = chunk[:, :, :, :].rearrange("p r b j -> p (r b j)")
        rin = ring[:, 0:U * D].rearrange("p (u d) -> p u d", u=U)
        rT = ring[:, 512:512 + U * P].rearrange("p (u d) -> p u d", u=U)
        hs = ring[:, 1024:1024 + U * F].rearrange("p (u f) -> p u f", u=U)
        hT = ring[:, 2048:2048 + U * F].rearrange("p (u f) -> p u f", u=U)
        ro = ring[:, 3072:3072 + U * D].rearrange("p (u d) -> p u d", u=U)
        back = [ring[:, 4096 + i * 1024:5120 + i * 1024].rearrange("p (k d) -> p k d", k=K * TB) for i in range(2)]
        zs = [ring[:, i:i + ROWS].rearrange("p (b d) -> p b d", b=TB) for i in (6144, 8192)]
        fin = [ring[:, 6656 + i * ROWS:6656 + (i + 1) * ROWS].rearrange("p (b d) -> p b d", b=TB) for i in range(2)]
        row_back = [ring[:, 7680 + i * K * TB:7680 + (i + 1) * K * TB].bitcast(I32) for i in range(2)]
        moved = ring[:, 13312:13312 + GROUPS * K * TB * (E - 1)].rearrange("p (r e) -> p r e", e=E - 1)
        move = ring[:, 15360:15360 + GROUPS * K * TB]
        many = ring[0:1, 8192:8192 + PACKS * E].rearrange("p (t e) -> p t e", e=E)
        pack_e = ring[0:1, 11264:11264 + PACKS]
        pack_s = ring[0:1, 11456:11456 + PACKS]
        over = ring[:, 12288:12288 + E * (N // PR)].rearrange("p (e k) -> p e k", e=E)

        tp = [ctx.enter_context(nc.psum_tensor(f"tp{i}", [P, 2 * ROWS], F32)) for i in range(2)]
        acc = ctx.enter_context(nc.psum_tensor("acc", [P, ROWS], F32))
        sp_ = [ctx.enter_context(nc.psum_tensor(f"spare{i}", [P, ROWS], F32)) for i in range(2)]
        misc = ctx.enter_context(nc.psum_tensor("misc", [P, ROWS], F32))
        bank_x = [tp[0][:, 0:ROWS], tp[1][:, 0:ROWS], acc[:, :], sp_[0][:, :]]
        bank_y = [tp[0][:, ROWS:2 * ROWS], tp[1][:, ROWS:2 * ROWS], misc[:, :], sp_[1][:, :]]

        loaded = [sem(f"chunk_loaded{i}") for i in range(RING)]
        weights_in = sem("weights_in")
        x_in = sem("x_in")
        masked = sem("masked")
        logged = sem("logged")
        inverted = sem("inverted")
        squared = sem("squared")
        turned = sem("turned")
        weighted = sem("weighted")
        added = sem("added")
        accT_out = sem("accT_out")
        blank = sem("blank")
        zeros_ok = sem("zeros_ok")
        const_ok = sem("const_ok")
        vec = sem("vector_step")
        mv_ready = sem("mv_ready")
        lnv_ready = sem("lnv_ready")
        guessed = sem("guessed")
        z_ready = sem("z_ready")
        rs_ready = sem("rs_ready")
        zn_ready = sem("zn_ready")
        z_free = sem("z_free")
        ln_ready = sem("ln_ready")
        misc_full = sem("misc_full")
        misc_read = sem("misc_read")
        hot_ready = sem("hot_ready")
        diff_ready = sem("diff_ready")
        exp_ready = sem("exp_ready")
        rows_ready = sem("rows_ready")
        carried = sem("carried")
        scattered = sem("scattered")
        y_free = sem("y_free")
        table_ready = sem("table_ready")
        spare_zero = sem("spare_zero")
        padded = sem("padded")
        ends_ready = sem("ends_ready")
        rin_full = [sem(f"rin_full{h}") for h in range(2)]
        rin_turned = sem("rin_turned")
        rT_ready = sem("rT_ready")
        hid_full = sem("hid_full")
        hs_ready = sem("hs_ready")
        hid_turned = sem("hid_turned")
        hT_ready = sem("hT_ready")
        o_full = sem("o_full")
        ro_ready = sem("ro_ready")
        ro_out = [sem(f"ro_out{h}") for h in range(2)]
        idx_ready = sem("idx_ready")
        back_in = [sem(f"back_in{i}") for i in range(2)]
        fin_ready = sem("fin_ready")
        fin_free = sem("fin_free")
        stored = [sem(f"stored{i}") for i in range(2)]

        block = ctx.enter_context(nc.Block())

        W_DMAS = 9
        POOL_CONSTS = 8
        CONSTS = POOL_CONSTS + 4
        MISC = 4
        SETUP_MISC = 2

        def row(t):
            return t.rearrange("(a d) -> a d", a=1).partition_broadcast(P)

        def tile_experts(n, engine):
            _, values = nc.values_load_multi_w_load_instructions(
                w_tab[0:1, bass.ds(n * 2, 3)], engines=[engine], min_val=0, max_val=E - 1)
            return values

        def rows(t, g):
            return t[:, bass.ds(g * TB, TB), :] if len(t.shape) == 3 else t[:, bass.ds(g * TB, TB)]

        @block.sync
        def _(sp):
            sp.dma_start(xs[:, :, :], x_v).then_inc(x_in, 16)

            def load(g, c):
                sp.dma_start(chunk[:, c % RING, :, :],
                             adj_v[:, g, :, c * JC:(c + 1) * JC]).then_inc(loaded[c % RING], 16)

            sp.dma_start(wgs[:, :], gnn_w).then_inc(x_in, 16)
            sp.dma_start(bg_bc[:, :], row(gnn_b)).then_inc(x_in, 16)
            for c in range(RING):
                load(0, c)
            for dst, src in ((gws[:, :], gate_w),
                             (gb_bc[:, :], row(gate_b)),
                             (w1s[:, :, :], w1.rearrange("e h f -> h e f")),
                             (w2s[:, 0, :, :], w2[:, 0:P, :].rearrange("e f h -> f e h")),
                             (w2s[:, 1, :, :], w2[:, P:2 * P, :].rearrange("e f h -> f e h")),
                             (b1_bc[:, :, :].rearrange("p e f -> p (e f)"), row(b1.rearrange("e f -> (e f)"))),
                             (b2_bc[:, :, :].rearrange("p e d -> p (e d)"), row(b2.rearrange("e d -> (e d)"))),
                             (gamma_bc[:, :], row(gamma)),
                             (beta_bc[:, :], row(beta))):
                sp.dma_start(dst, src).then_inc(weights_in, 16)

            def group(g, last):
                for c in range(CHUNKS):
                    if last and c + RING >= CHUNKS:
                        break
                    sp.wait_ge(turned, (g * CHUNKS + c + 1) * PAIRS)
                    n = c + RING
                    load(g + n // CHUNKS, n % CHUNKS)

            with sp.Fori(0, GROUPS - 1) as g:
                group(g, False)
            group(GROUPS - 1, True)

            sp.wait_ge(ends_ready, 1)
            sp.wait_ge(zeros_ok, 2)
            with sp.Fori(0, E) as e:
                end = sp.value_load(ends[0:1, bass.ds(e, 1)], min_val=0, max_val=SPARE - PR)
                sp.dma_start(rows_in[bass.ds(end, PR), :].rearrange("(u p) d -> p u d", p=P),
                             zeros[:, :, :]).then_inc(padded, 16)
            sp.wait_ge(table_ready, 1)
            sp.wait_ge(y_free, GROUPS + 1)
            sp.wait_ge(spare_zero, E * 16)
            sp.wait_ge(padded, E * 16)
            with sp.Fori(0, TURNS) as n:
                for h in range(2):
                    r = sp.value_load(r_tab[0:1, bass.ds(2 * n + h, 1)], min_val=0, max_val=SPARE + (E - 1) * PR)
                    sp.wait_ge(rin_turned, n * U + (h + 1) * H)
                    sp.dma_start(rin[:, h * H:(h + 1) * H, :],
                                 rows_in[bass.ds(r, PR), :].rearrange("(u p) d -> p u d", p=P)).then_inc(rin_full[h], 16)

            sp.sem_inc(fin_free, 2)
            with sp.Fori(0, GROUPS // 2) as n:
                for i in range(2):
                    sp.wait_ge(fin_ready, 2 * n + i + 1)
                    sp.dma_start(out_v[:, 2 * n + i, :, :], fin[i]).then_inc(stored[i], 16)
                for i in range(2):
                    sp.wait_ge(stored[i], (n + 1) * 16)
                    sp.sem_inc(fin_free, 1)
            for i in range(2):
                sp.wait_ge(stored[i], GROUPS // 2 * 16)

        @block.gpsimd
        def _(pool):
            pool.memset(ident[:, :], 0.0).then_inc(blank, 1)
            pool.memset(before[:, :], 1.0).then_inc(blank, 1)
            pool.memset(ones[:, :], 1.0).then_inc(const_ok, 1)
            pool.memset(tiny[:, :], TINY).then_inc(const_ok, 1)
            pool.memset(zeros[:, :, :], 0.0).then_inc(zeros_ok, 1)
            pool.memset(pool_carrier[:, :], 0.0).then_inc(zeros_ok, 1)
            pool.iota(iota_e[:, :], pattern=[[1, E]], base=0, channel_multiplier=0,
                      allow_small_or_imprecise_dtypes=True).then_inc(const_ok, 1)
            pool.iota(region0[:, :], pattern=[[REGION, E]], base=0, channel_multiplier=0,
                      allow_small_or_imprecise_dtypes=True).then_inc(const_ok, 1)
            pool.iota(pack_steps[:, :], pattern=[[PR, N // PR]], base=0, channel_multiplier=0,
                      allow_small_or_imprecise_dtypes=True).then_inc(const_ok, 1)
            pool.iota(pack_no[:, :], pattern=[[1, PACKS]], base=0, channel_multiplier=0,
                      allow_small_or_imprecise_dtypes=True).then_inc(const_ok, 1)
            pool.wait_ge(blank, 2)
            pool.affine_select(out=ident[:, :], in_=ident[:, :], compare_op=ALU.not_equal, fill=1.0,
                               base=0, pattern=[[-1, P]], channel_multiplier=1).then_inc(const_ok, 1)
            pool.affine_select(out=before[:, :], in_=before[:, :], compare_op=ALU.is_gt, fill=0.0,
                               base=0, pattern=[[1, P]], channel_multiplier=-1).then_inc(const_ok, 1)
            pool.wait_ge(zeros_ok, 2)
            for e in range(E):
                pool.dma_start(rows_in[SPARE + e * PR:SPARE + (e + 1) * PR, :].rearrange("(u p) d -> p u d", p=P),
                               zeros[:, :, :]).then_inc(spare_zero, 16)

            def carry():
                pool.tensor_tensor(pool_carrier[0:1, 0:1], pool_carrier[0:1, 1:2], pool_carrier[0:1, 2:3],
                                   ALU.mult).then_inc(carried, 1)

            pool.sem_inc(y_free, 1)
            pool.sem_inc(carried, 1)
            with pool.Fori(0, GROUPS) as g:
                pool.wait_ge(carried, g + 1)
                pool.wait_ge(rows_ready, g + 1)
                carry()
                for k in range(K):
                    for b in range(TB):
                        pool.indirect_dma_start(
                            rows_in, bass.IndirectOffsetOnAxis(row_now[:, k, b:b + 1].bitcast(U32), 0),
                            y[:, b, :], None).then_inc(scattered, 16)
                pool.wait_ge(scattered, (g + 1) * K * TB * 16)
                pool.sem_inc(y_free, 1)

            with pool.Fori(0, TURNS) as n:
                for h in range(2):
                    pool.wait_ge(ro_ready, n * U + (h + 1) * H)
                    pool.dma_start(results_v[:, bass.ds(2 * n + h, 1), :, :].rearrange("p a u d -> p (a u) d"),
                                   ro[:, h * H:(h + 1) * H, :]).then_inc(ro_out[h], 16)

            with pool.Fori(0, GROUPS // 2) as n:
                for i in range(2):
                    pool.wait_ge(carried, GROUPS + 2 * n + i + 1)
                    pool.wait_ge(idx_ready, 2 * n + i + 1)
                    carry()
                    for kb in range(K * TB):
                        pool.indirect_dma_start(
                            back[i][:, kb, :], None, rows_out,
                            bass.IndirectOffsetOnAxis(row_back[i][:, kb:kb + 1].bitcast(U32), 0)).then_inc(back_in[i], 16)

        @block.scalar
        def _(act):
            act.preload_act_table_set("natural_log_exp_and_others")
            act.sem_inc(weighted, 2)
            act.wait_ge(const_ok, CONSTS)

            def two(c):
                return chunk[:, c % RING:c % RING + 2, :, :]

            def log(g, c):
                act.wait_ge(masked, g * CHUNKS + c + 2)
                act.activation(two(c), two(c), ACT.Ln, bias=tiny[:, 0:1]).then_inc(logged, 1)

            def invert(g, c):
                act.wait_ge(logged, g * (CHUNKS // 2) + c // 2 + 1)
                act.activation(two(c), two(c), ACT.Exp, scale=-1.0).then_inc(inverted, 1)

            def weigh(g, m):
                act.wait_ge(turned, g * PPG + m + 1)
                act.wait_ge(added, g * PPG + m + 1)
                act.activation(wT[:, m % WSLOTS, :], tp[m % 2][:, :], ACT.Exp, bias=minus2[:, 0:1],
                               scale=-2.0).then_inc(weighted, 1)

            def guess(j, i):
                act.wait_ge(mv_ready, j + 1)
                act.activation(lnv[:, :], mv_now[:, i, :, 1], ACT.Ln, bias=eps[:, 0:1]).then_inc(lnv_ready, 1)
                act.wait_ge(lnv_ready, j + 1)
                act.activation(rs[:, i, :], lnv[:, :], ACT.Exp, scale=-0.5).then_inc(guessed, 1)

            def gate_slot(g, m):
                if m == 4:
                    guess(GROUPS + g, 0)
                if m == 16:
                    soften(g)

            def soften(g):
                act.wait_ge(diff_ready, g + 1)
                act.activation(ed[:, :], dv[:, :], ACT.Exp).then_inc(exp_ready, 1)

            def group(g, gate, last):
                for m in range(PPG):
                    c, k = divmod(m, PAIRS)
                    weigh(g, m)
                    n = m // (2 * PAIRS) * 2 + LOG_LEAD
                    if m % 2 and not (last and n >= CHUNKS):
                        (log if m % (2 * PAIRS) == 1 else invert)(g + n // CHUNKS, n % CHUNKS)
                    if gate:
                        gate_slot(g - 1, m)
                    elif k == 0 and c + 2 < GROUPS:
                        guess(c + 2, 0)

            log(0, 0)
            invert(0, 0)
            for j in range(2):
                guess(j, 0)
            log(0, 2)
            invert(0, 2)
            group(0, False, False)
            with act.Fori(1, GROUPS - 1) as g:
                group(g, True, False)
            group(GROUPS - 1, True, True)
            for m in range(PPG):
                gate_slot(GROUPS - 1, m)

            def copy_rows(n, h):
                for i in range(H):
                    u = (h % 2) * H + i
                    act.wait_ge(rin_turned, U + n * U + h * H + i + 1)
                    act.activation(rT[:, u, :], bank_x[u][:, 0:P], ACT.Copy).then_inc(rT_ready, 1)

            def relu_hidden(n, h):
                for i in range(H):
                    u = (h % 2) * H + i
                    act.wait_ge(hid_turned, n * U + h * H + i + 1)
                    act.activation(hT[:, u, :], bank_x[u][:, P:P + F], ACT.Relu).then_inc(hT_ready, 1)

            def step(n, last):
                copy_rows(n, 1)
                relu_hidden(n, 0)
                if not last:
                    copy_rows(n, 2)
                relu_hidden(n, 1)

            copy_rows(0, 0)
            with act.Fori(0, TURNS - 1) as n:
                step(n, False)
            step(TURNS - 1, True)

            def first_norm(g, i, first=False):
                if not first:
                    act.wait_ge(fin_ready, g - 1)
                for b in range(TB):
                    ins = act.activation(zs[i][:, b, :], rows(xs, g)[:, b, :], ACT.Identity,
                                         bias=rows(shift_all, g)[:, b:b + 1], scale=rows(rstd, g)[:, b:b + 1])
                ins.then_inc(z_ready, 1)

            def second_norm(g, i):
                act.wait_ge(rs_ready, g + 1)
                for b in range(TB):
                    ins = act.activation(zs[i][:, b, :], zs[i][:, b, :], ACT.Identity,
                                         bias=shift[:, i, b:b + 1], scale=rs[:, i, b:b + 1])
                ins.then_inc(zn_ready, 1)

            act.wait_ge(z_free, 1)
            for i in range(2):
                first_norm(i, i, True)
            guess(2 * GROUPS, 0)
            with act.Fori(0, GROUPS // 2 - 1) as n:
                for i in range(2):
                    second_norm(2 * n + i, i)
                    guess(2 * GROUPS + 2 * n + i + 1, 1 - i)
                    first_norm(2 * n + i + 2, i)
            second_norm(GROUPS - 2, 0)
            guess(3 * GROUPS - 1, 1)
            second_norm(GROUPS - 1, 1)

        @block.vector
        def _(dve):
            steps = [0]

            def plain_next():
                dve.tensor_copy(carrier[0:1, 1:2], carrier[0:1, 0:1])

            def link(ins, base, plain=False):
                steps[0] += 1
                ins.then_inc(vec, 1)
                dve.wait_ge(vec, base + steps[0])
                if plain:
                    plain_next()

            def slot(c):
                return chunk[:, c % RING, :, :]

            def mask(g, c):
                dve.wait_ge(loaded[c % RING], (g * (CHUNKS // RING) + c // RING + 1) * 16)
                dve.scalar_tensor_tensor(out=slot(c), in0=slot(c), scalar=1.0, in1=slot(c),
                                         op0=ALU.is_lt, op1=ALU.mult).then_inc(masked, 1)

            def square(g, c):
                dve.wait_ge(inverted, g * (CHUNKS // 2) + c // 2 + 1)
                dve.scalar_tensor_tensor(out=slot(c), in0=slot(c), scalar=2.0, in1=slot(c),
                                         op0=ALU.subtract, op1=ALU.mult).then_inc(squared, 1)

            def rows_stats(src, i, base):
                plain_next()
                for b in range(TB):
                    ins = dve.bn_stats(stats[:, b, :], src[:, b, :])
                link(ins, base, plain=True)
                for b in range(TB):
                    ins = dve.bn_aggr(mv_now[:, i, b, :], stats[:, b, :])
                ins.then_inc(mv_ready, 1)

            def refine(j, i, base):
                dve.wait_ge(guessed, j + 1)
                link(dve.scalar_tensor_tensor(out=nt[:, :], in0=mv_now[:, i, :, 1], scalar=EPS, in1=rs[:, i, :],
                                              op0=ALU.add, op1=ALU.mult), base)
                link(dve.tensor_tensor(nt[:, :], nt[:, :], rs[:, i, :], ALU.mult), base)
                link(dve.tensor_scalar(nt[:, :], nt[:, :], -0.5, 1.5, ALU.mult, ALU.add), base)
                link(dve.tensor_tensor(rs[:, i, :], rs[:, i, :], nt[:, :], ALU.mult), base)

            def normalise(src, dst):
                for b in range(TB):
                    ins = dve.tensor_scalar(dst[:, b, :], src[:, b, :], mv_now[:, 0, b, 0:1], rs[:, 0, b:b + 1],
                                            ALU.subtract, ALU.mult)
                ins.then_inc(ln_ready, 1)

            dve.memset(w_tab[:, :], 0).then_inc(const_ok, 1)
            dve.memset(minus2[:, :], -2.0).then_inc(const_ok, 1)
            dve.memset(eps[:, :], EPS).then_inc(const_ok, 1)
            dve.memset(carrier[:, :], 0.0).then_inc(const_ok, 1)
            dve.wait_ge(const_ok, CONSTS)
            for c in range(3):
                mask(0, c)

            dve.sem_inc(misc_read, 1)
            dve.wait_ge(x_in, 3 * 16)
            NORM_STEPS = 5

            def norm_stats(j):
                steps[0] = 0
                rows_stats(rows(xs, j), 0, j * NORM_STEPS)

            def norm_rows(j):
                refine(j, 0, j * NORM_STEPS)
                normalise(rows(xs, j), y)

            def keep_turned(j):
                dve.wait_ge(misc_full, j * SETUP_MISC + 1)
                dve.tensor_copy(yT[:, :], misc[:, :]).then_inc(misc_read, 1)

            def keep_messages(j):
                dve.wait_ge(misc_full, j * SETUP_MISC + 2)
                dve.tensor_tensor(rows(msg, j), misc[:, :].rearrange("p (b d) -> p b d", b=TB),
                                  bg_bc[:, :].unsqueeze(1).to_broadcast([P, TB, D]), ALU.add).then_inc(misc_read, 1)

            def message_slot(m):
                c, k = divmod(m, PAIRS)
                if k == 0 and c + 1 < GROUPS:
                    keep_turned(c + 1)
                if k == 0 and c + 2 < GROUPS:
                    norm_stats(c + 2)
                if k == 1 and c + 2 < GROUPS:
                    norm_rows(c + 2)
                if k == 1 and c + 1 < GROUPS:
                    keep_messages(c + 1)

            norm_stats(0)
            norm_rows(0)
            norm_stats(1)
            keep_turned(0)
            norm_rows(1)
            keep_messages(0)

            for c in range(3, MASK_LEAD):
                mask(0, c)
            for c in range(SQUARE_LEAD):
                square(0, c)
            SETUP_ALL = GROUPS * NORM_STEPS
            GATE_STEPS = 11

            def spread(t, shape):
                return t.to_broadcast(shape)

            def gate_sum(g):
                dve.wait_ge(added, (g + 1) * PPG + WSLOTS)
                dve.tensor_copy(accT[:, :], acc[:, :]).then_inc(accT_out, 1)

            def gate_base(g):
                return SETUP_ALL + 1 + g * (NORM_STEPS + GATE_STEPS)

            def done(ins):
                steps[0] += 1
                ins.then_inc(vec, 1)

            def gate_slot(g, m):
                base = gate_base(g)
                results = SETUP_MISC * GROUPS + g * MISC

                def need():
                    dve.wait_ge(vec, base + steps[0])

                if m == 2:
                    steps[0] = 0
                    dve.wait_ge(misc_full, results + 1)
                    dve.tensor_tensor(rows(xs, g), misc[:, :].rearrange("p (b d) -> p b d", b=TB),
                                      rows(xs, g), ALU.add).then_inc(misc_read, 1)
                if m == 3:
                    dve.wait_ge(misc_read, 1 + results + 1)
                    rows_stats(rows(xs, g), 0, base)
                if m == 6:
                    refine(GROUPS + g, 0, base)
                    dve.wait_ge(y_free, g + 1)
                    normalise(rows(xs, g), y)
                    dve.tensor_copy(rows(mv, g), mv_now[:, 0, :, :])
                    done(dve.tensor_copy(rows(rstd, g), rs[:, 0, :]))
                if m == 8:
                    dve.wait_ge(misc_full, results + 2)
                    dve.tensor_copy(yT[:, :], misc[:, :]).then_inc(misc_read, 1)
                if m == 11:
                    dve.wait_ge(misc_full, results + 3)
                    dve.tensor_tensor(logits[:, :, :], misc[:, 0:TB * E].rearrange("p (b e) -> p b e", b=TB),
                                      gb_bc[:, :].unsqueeze(1).to_broadcast([P, TB, E]), ALU.add).then_inc(misc_read, 1)
                if m == 12:
                    dve.wait_ge(misc_read, 1 + results + 3)
                    plain_next()
                    for b in range(TB):
                        ins = dve.max(top8[:, b, :], logits[:, b, :])
                    done(ins)
                if m == 13:
                    need()
                    plain_next()
                    for b in range(TB):
                        ins = dve.max_index(idx8[:, b, :], top8[:, b, :], logits[:, b, :])
                    done(ins)
                if m == 14:
                    need()
                    dve.tensor_tensor(dv[:, :], top8[:, :, 1], top8[:, :, 0], ALU.subtract).then_inc(diff_ready, 1)
                    done(dve.tensor_copy(idxf[:, :, :], idx8[:, :, 0:K]))
                if m == 15:
                    need()
                    for k in range(K):
                        ins = dve.tensor_tensor(hot[:, k, :, :], iota_e[:, :].unsqueeze(1).to_broadcast([P, TB, E]),
                                                idxf[:, :, k:k + 1].to_broadcast([P, TB, E]), ALU.is_equal)
                    done(ins)
                if m == 16:
                    need()
                    dve.tensor_tensor(both[:, :, :], hot[:, 0, :, :], hot[:, 1, :, :], ALU.add).then_inc(hot_ready, 1)
                if m == 19:
                    dve.wait_ge(misc_full, results + 4)
                    done(dve.tensor_tensor(rank[:, :, :], misc[:, 0:TB * E].rearrange("p (b e) -> p b e", b=TB),
                                           nexts[:, :].unsqueeze(1).to_broadcast([P, TB, E]), ALU.add))
                if m == 20:
                    need()
                    dve.tensor_tensor(nexts[:, :], misc[:, TB * E:(TB + 1) * E], nexts[:, :], ALU.add).then_inc(misc_read, 1)
                    done(dve.tensor_tensor(picked[:, :, :, :], hot[:, :, :, :],
                                           rank[:, :, :].unsqueeze(1).to_broadcast([P, K, TB, E]), ALU.mult))
                if m == 21:
                    need()
                    done(dve.reduce_sum(rowf[:, :, :], picked[:, :, :, :], AX.X))
                if m == 22:
                    need()
                    dve.tensor_copy(row_all[:, bass.ds(g, 1), :].rearrange("p a k -> p (a k)"),
                                    rowf[:, :, :].rearrange("p k b -> p (k b)"))
                    dve.tensor_copy(row_now[:, :, :], rowf[:, :, :]).then_inc(rows_ready, 1)
                if m == 23:
                    dve.wait_ge(exp_ready, g + 1)
                    done(dve.tensor_scalar(dv[:, :], ed[:, :], 1.0, None, ALU.add))
                if m == 24:
                    need()
                    done(dve.reciprocal(dv[:, :], dv[:, :]))
                if m == 25:
                    need()
                    dve.tensor_copy(rows(share, g)[:, :, 0], dv[:, :])
                    done(dve.tensor_tensor(rows(share, g)[:, :, 1], ed[:, :], dv[:, :], ALU.mult))
                if m == 26:
                    need()
                    assert steps[0] == NORM_STEPS + GATE_STEPS

            def group(g, gate, last):
                if gate:
                    gate_sum(g - 1)
                for m in range(PPG):
                    turn, k = divmod(m, 2 * PAIRS)
                    n = 2 * turn + k // 2 + (MASK_LEAD if k % 2 == 0 else SQUARE_LEAD)
                    if not (last and n >= CHUNKS):
                        (mask if k % 2 == 0 else square)(g + n // CHUNKS, n % CHUNKS)
                    if gate:
                        gate_slot(g - 1, m)
                    else:
                        message_slot(m)

            group(0, False, False)
            dve.wait_ge(weights_in, W_DMAS * 16)
            dve.tensor_copy(nexts[:, :], region0[:, :]).then_inc(vec, 1)
            dve.wait_ge(vec, SETUP_ALL + 1)
            with dve.Fori(1, GROUPS - 1) as g:
                group(g, True, False)
            group(GROUPS - 1, True, True)
            gate_sum(GROUPS - 1)
            for m in range(PPG):
                gate_slot(GROUPS - 1, m)

            base = gate_base(GROUPS)
            steps[0] = 0
            dve.tensor_copy(ends[:, :], nexts[0:1, :]).then_inc(ends_ready, 1)
            link(dve.tensor_tensor(count[:, :], nexts[:, :], region0[:, :], ALU.subtract), base)
            NB = N // PR
            link(dve.tensor_tensor(over, count[:, :].unsqueeze(2).to_broadcast([P, E, NB]),
                                   pack_steps[:, :].unsqueeze(1).to_broadcast([P, E, NB]), ALU.is_gt), base)
            link(dve.reduce_sum(packs_of[:, :], over, AX.X), base)
            upto, step = packs_of, 1
            while step < E:
                to = packs_to[0] if upto is not packs_to[0] else packs_to[1]
                dve.tensor_copy(to[:, 0:step], upto[:, 0:step])
                link(dve.tensor_tensor(to[:, step:E], upto[:, step:E], upto[:, 0:E - step], ALU.add), base)
                upto, step = to, 2 * step
            link(dve.tensor_tensor(many, upto[0:1, :].unsqueeze(1).to_broadcast([1, PACKS, E]),
                                   pack_no[:, :].unsqueeze(2).to_broadcast([1, PACKS, E]), ALU.is_le), base)
            link(dve.reduce_sum(pack_e, many, AX.X), base)
            link(dve.tensor_tensor(many, many, packs_of[0:1, :].unsqueeze(1).to_broadcast([1, PACKS, E]), ALU.mult), base)
            link(dve.reduce_sum(pack_s, many, AX.X), base)
            link(dve.tensor_tensor(pack_s, pack_no[:, :], pack_s, ALU.subtract), base)
            link(dve.tensor_scalar(w_tab[:, 1:1 + PACKS], pack_e, float(E - 1), None, ALU.min), base)
            link(dve.tensor_scalar(pack_e, pack_e, float(REGION), None, ALU.mult), base)
            dve.scalar_tensor_tensor(out=r_tab[:, :], in0=pack_s, scalar=float(PR), in1=pack_e,
                                     op0=ALU.mult, op1=ALU.add).then_inc(table_ready, 1)
            dve.wait_ge(table_ready, 1)
            link(dve.scalar_tensor_tensor(out=shift_all[:, :], in0=mv[:, :, 0], scalar=-1.0, in1=rstd[:, :],
                                          op0=ALU.mult, op1=ALU.mult), base)
            dve.sem_inc(z_free, 1)
            link(dve.tensor_scalar(packs_of[:, :], packs_of[:, :], float(PR), -float(REGION), ALU.mult, ALU.add), base)
            rows_flat = row_all[:, :, :].rearrange("p g k -> p (g k)")
            wide = [P, GROUPS * K * TB, E - 1]
            link(dve.tensor_tensor(moved, rows_flat.unsqueeze(2).to_broadcast(wide),
                                   region0[:, 1:E].unsqueeze(1).to_broadcast(wide), ALU.is_ge), base)
            link(dve.tensor_tensor(moved, moved, packs_of[:, 0:E - 1].unsqueeze(1).to_broadcast(wide), ALU.mult), base)
            link(dve.reduce_sum(move, moved, AX.X), base)
            link(dve.tensor_tensor(rows_flat, rows_flat, move, ALU.add), base)

            def bias_hidden(n, h):
                for i in range(H):
                    u = (h % 2) * H + i
                    e = experts[h + 1]
                    dve.wait_ge(hid_full, n * U + h * H + i + 1)
                    dve.tensor_tensor(hs[:, u, :], bank_y[u][:, P:P + F],
                                      b1_bc[:, bass.ds(e, 1), :].rearrange("p a f -> p (a f)"), ALU.add).then_inc(hs_ready, 1)

            def bias_output(n, h, first=False):
                for i in range(H):
                    u = (h % 2) * H + i
                    e = experts[h + 1]
                    dve.wait_ge(o_full, n * U + h * H + i + 1)
                    if i == 0 and not first:
                        dve.wait_ge(ro_out[h % 2], (n + h) * 16)
                    dve.tensor_tensor(ro[:, u, :], bank_y[u][:, 0:D],
                                      b2_bc[:, bass.ds(e, 1), :].rearrange("p a d -> p (a d)"), ALU.add).then_inc(ro_ready, 1)

            experts = []

            def step(n, kind):
                experts[:] = tile_experts(n, mybir.EngineType.DVE)
                bias_hidden(n, 0)
                if kind != "first":
                    bias_output(n, -1, kind == "second")
                bias_hidden(n, 1)
                bias_output(n, 0, kind == "first")

            step(0, "first")
            step(1, "second")
            with dve.Fori(2, TURNS) as n:
                step(n, "middle")
            experts[:] = tile_experts(TURNS, mybir.EngineType.DVE)
            bias_output(TURNS, -1)

            for h in range(2):
                dve.wait_ge(ro_out[h], TURNS * 16)
            for i in range(2):
                dve.tensor_copy(row_back[i], row_all[:, i, :]).then_inc(idx_ready, 1)
            LIST_STEPS = steps[0]
            last_base = base + LIST_STEPS
            COMBINE_STEPS, TURN_STEPS = 3, 9

            def combine(g, i, n, more, base):
                z = zs[i]
                dve.wait_ge(z_ready, g + 1)
                dve.wait_ge(back_in[i], (n + 1) * K * TB * 16)
                for k in range(K):
                    for b in range(TB):
                        ins = dve.scalar_tensor_tensor(out=z[:, b, :], in0=back[i][:, k * TB + b, :],
                                                       scalar=rows(share, g)[:, b, k:k + 1], in1=z[:, b, :],
                                                       op0=ALU.mult, op1=ALU.add)
                    link(ins, base)
                if more:
                    dve.tensor_copy(row_back[i], row_all[:, bass.ds(g + 2, 1), :].rearrange("p a k -> p (a k)")).then_inc(idx_ready, 1)
                rows_stats(z, i, base)

            def to_scalar(i):
                dve.scalar_tensor_tensor(out=shift[:, i, :], in0=mv_now[:, i, :, 0], scalar=-1.0, in1=rs[:, i, :],
                                         op0=ALU.mult, op1=ALU.mult).then_inc(rs_ready, 1)

            def finish(g, i, base):
                z = zs[i]
                dve.wait_ge(zn_ready, g + 1)
                link(dve.tensor_tensor(z, z, gamma_bc[:, :].unsqueeze(1).to_broadcast([P, TB, D]), ALU.mult), base)
                link(dve.tensor_tensor(z, z, beta_bc[:, :].unsqueeze(1).to_broadcast([P, TB, D]), ALU.add), base)
                dve.wait_ge(fin_free, g + 1)
                dve.tensor_tensor(fin[i], z, rows(xs, g), ALU.add).then_inc(fin_ready, 1)

            def last_turn(g, i, n, more):
                base = last_base + COMBINE_STEPS + g * TURN_STEPS
                steps[0] = 0
                refine(2 * GROUPS + g, i, base)
                to_scalar(i)
                combine(g + 1, 1 - i, n + i, more, base)
                finish(g, i, base)
                assert steps[0] == TURN_STEPS

            steps[0] = 0
            combine(0, 0, 0, True, last_base)
            with dve.Fori(0, GROUPS // 2 - 2) as n:
                last_turn(2 * n, 0, n, True)
                last_turn(2 * n + 1, 1, n, True)
            last_turn(GROUPS - 4, 0, GROUPS // 2 - 2, True)
            last_turn(GROUPS - 3, 1, GROUPS // 2 - 2, False)
            g = GROUPS - 2
            last_turn(g, 0, g // 2, False)
            base = last_base + COMBINE_STEPS + (g + 1) * TURN_STEPS
            steps[0] = 0
            refine(2 * GROUPS + g + 1, 1, base)
            to_scalar(i=1)
            finish(g + 1, 1, base)

        @block.tensor
        def _(pe):
            pe.sem_inc(added, WSLOTS)
            pe.wait_ge(const_ok, CONSTS)
            pe.wait_ge(x_in, 3 * 16)

            def turn_rows():
                for b in range(TB):
                    ins = pe.transpose(misc[:, b * P:(b + 1) * P], y[:, b, :], ident[:, :])
                ins.then_inc(misc_full, 1)

            def message_turn(j):
                pe.wait_ge(misc_read, 1 + j * SETUP_MISC)
                pe.wait_ge(ln_ready, j + 1)
                turn_rows()

            def message_products(j):
                pe.wait_ge(misc_read, 1 + j * SETUP_MISC + 1)
                for b in range(TB):
                    ins = pe.matmul(misc[:, b * D:(b + 1) * D], yT[:, b * P:(b + 1) * P], wgs[:, :],
                                    start=True, stop=True)
                ins.then_inc(misc_full, 1)

            message_turn(0)
            message_products(0)

            def gate_sum(g):
                pe.wait_ge(misc_read, 1 + SETUP_MISC * GROUPS + g * MISC)
                for b in range(TB):
                    ins = pe.transpose(misc[:, b * P:(b + 1) * P], accT[:, b * P:(b + 1) * P], ident[:, :])
                ins.then_inc(misc_full, 1)

            def gate_turn(g):
                pe.wait_ge(ln_ready, GROUPS + g + 1)
                turn_rows()

            def gate_logits(g):
                pe.wait_ge(misc_read, 1 + SETUP_MISC * GROUPS + g * MISC + 2)
                for b in range(TB):
                    ins = pe.matmul(misc[:, b * E:(b + 1) * E], yT[:, b * P:(b + 1) * P], gws[:, :],
                                    start=True, stop=True)
                ins.then_inc(misc_full, 1)

            def gate_ranks(g):
                pe.wait_ge(hot_ready, g + 1)
                flat = both[:, :, :].rearrange("p b e -> p (b e)")
                pe.matmul(misc[:, 0:TB * E], before[:, :], flat, start=True, stop=False, skip_group_check=True)
                for d in range(1, TB):
                    pe.matmul(misc[:, d * E:TB * E], ones[:, :], flat[:, 0:(TB - d) * E], start=False,
                              stop=(d == TB - 1), skip_group_check=True)
                for b in range(TB):
                    ins = pe.matmul(misc[:, TB * E:(TB + 1) * E], ones[:, :], flat[:, b * E:(b + 1) * E],
                                    start=(b == 0), stop=(b == TB - 1), skip_group_check=True)
                ins.then_inc(misc_full, 1)

            def group(g, gate, last):
                def products(m):
                    pe.wait_ge(weighted, g * PPG + m + 1 + 2)
                    if gate and m == 0:
                        pe.wait_ge(accT_out, g)
                    if not gate and m % PAIRS == 0:
                        pe.wait_ge(misc_read, 1 + (m // PAIRS + 1) * SETUP_MISC)
                    for k in range(2):
                        n = 2 * m + k
                        ins = pe.matmul(acc[:, :], msg[:, n, :], wT[:, m % WSLOTS, k * ROWS:(k + 1) * ROWS],
                                        start=(n == 0), stop=(n == 2 * PPG - 1))
                    ins.then_inc(added, 1)

                for m in range(PPG):
                    c, k = divmod(m, PAIRS)
                    if k == 0:
                        pe.wait_ge(squared, g * CHUNKS + c + 1)
                    pe.wait_ge(weighted, g * PPG + m + 1)
                    for t in range(2):
                        for b in range(TB):
                            j = (2 * k + t) * P
                            ins = pe.transpose(tp[m % 2][:, t * ROWS + b * P:t * ROWS + (b + 1) * P],
                                               chunk[:, c % RING, b, j:j + P], ident[:, :])
                    ins.then_inc(turned, 1)
                    if m:
                        products(m - 1)
                    if not gate and c + 1 < GROUPS:
                        (message_turn if k == 0 else message_products)(c + 1)
                    if gate and m == 1:
                        gate_sum(g - 1)
                    if gate and m == 7:
                        gate_turn(g - 1)
                    if gate and m == 10:
                        gate_logits(g - 1)
                    if gate and m == 17:
                        gate_ranks(g - 1)
                products(PPG - 1)

            group(0, False, False)
            pe.wait_ge(weights_in, W_DMAS * 16)
            with pe.Fori(1, GROUPS - 1) as g:
                group(g, True, False)
            g = GROUPS - 1
            group(g, True, True)
            pe.wait_ge(accT_out, GROUPS)
            gate_sum(g)
            gate_turn(g)
            gate_logits(g)
            gate_ranks(g)

            pe.sem_inc(rin_turned, U)
            pe.wait_ge(misc_read, 1 + SETUP_MISC * GROUPS + GROUPS * MISC)
            pe.wait_ge(table_ready, 1)
            def turn_tile(n, h, first=False):
                for i in range(H):
                    u = (h % 2) * H + i
                    if not first:
                        pe.wait_ge(hT_ready, n * U + h * H + i + 1 - U)
                    pe.wait_ge(rin_full[h % 2], (n + 1 + h // 2) * 16)
                    pe.transpose(bank_x[u][:, 0:P], rin[:, u, :], ident[:, :]).then_inc(rin_turned, 1)

            def hidden(n, h, first=False):
                for i in range(H):
                    u = (h % 2) * H + i
                    e = experts[h + 1]
                    if not first:
                        pe.wait_ge(ro_ready, n * U + h * H + i + 1 - U)
                    pe.wait_ge(rT_ready, n * U + h * H + i + 1)
                    pe.matmul(bank_y[u][:, P:P + F], rT[:, u, :],
                              w1s[:, bass.ds(e, 1), :].rearrange("p a f -> p (a f)"),
                              start=True, stop=True).then_inc(hid_full, 1)

            def turn_hidden(n, h):
                for i in range(H):
                    u = (h % 2) * H + i
                    pe.wait_ge(hs_ready, n * U + h * H + i + 1)
                    for t in range(FT):
                        ins = pe.transpose(bank_x[u][:, P + t * P:P + (t + 1) * P], hs[:, u, t * P:(t + 1) * P],
                                           ident[:, :])
                    ins.then_inc(hid_turned, 1)

            def output(n, h):
                for i in range(H):
                    u = (h % 2) * H + i
                    e = experts[h + 1]
                    pe.wait_ge(hT_ready, n * U + h * H + i + 1)
                    for t in range(FT):
                        ins = pe.matmul(bank_y[u][:, 0:D], hT[:, u, t * P:(t + 1) * P],
                                        w2s[:, t, bass.ds(e, 1), :].rearrange("p a d -> p (a d)"),
                                        start=(t == 0), stop=(t == FT - 1))
                    ins.then_inc(o_full, 1)

            experts = []

            def step(n, kind):
                experts[:] = tile_experts(n, mybir.EngineType.PE)
                hidden(n, 0, kind == "first")
                if kind != "first":
                    output(n, -1)
                turn_tile(n, 1, kind == "first")
                turn_hidden(n, 0)
                hidden(n, 1, kind == "first")
                output(n, 0)
                if kind != "last":
                    turn_tile(n, 2)
                turn_hidden(n, 1)

            turn_tile(0, 0, True)
            step(0, "first")
            with pe.Fori(1, TURNS - 1) as n:
                step(n, "middle")
            step(TURNS - 1, "last")
            experts[:] = tile_experts(TURNS, mybir.EngineType.PE)
            output(TURNS, -1)

_INS = ['x', 'adj', 'L0_gnn_W', 'L0_gnn_B', 'L0_ffn_gate_w', 'L0_ffn_gate_b', 'L0_ffn_w1', 'L0_ffn_b1',
        'L0_ffn_w2', 'L0_ffn_b2', 'L0_ffn_gamma', 'L0_ffn_beta']
_OUTS = [((8192, 128), 'float32')]


def kernel(**inputs):
    import numpy as _np
    import concourse.bacc as _bacc
    from concourse import mybir as _mybir
    from concourse.bass_utils import run_bass_kernel_spmd as _run

    nc = _bacc.Bacc("TRN2", target_bir_lowering=False, num_devices=1)
    arrays, args = {}, []
    for name in _INS:
        a = _np.ascontiguousarray(inputs[name])
        arrays[f"in_{name}_dram"] = a
        args.append(nc.dram_tensor(f"in_{name}_dram", a.shape, _mybir.dt.from_np(a.dtype), kind="ExternalInput").ap())
    for i, (shape, dtype) in enumerate(_OUTS):
        dt = _mybir.dt.from_np(_np.dtype(dtype))
        args.append(nc.dram_tensor(f"out_{i}_dram", shape, dt, kind="ExternalOutput").ap())
    gnn_moe_kernel(nc, *args)
    r = _run(nc, [arrays], core_ids=[0])
    got = tuple(r.results[0][f"out_{i}_dram"] for i in range(len(_OUTS)))
    return got[0]
```
